# Optimizing a Trainium2 kernel written in Bass

```python
import numpy as np
import jax
import jax.numpy as jnp

def _softmax(x, axis=-1):
    return jax.nn.softmax(x, axis=axis)

def _gelu(x):
    return jax.nn.gelu(x, approximate=True)

def _silu(x):
    return jax.nn.silu(x)

def _sigmoid(x):
    return jax.nn.sigmoid(x)

def _layernorm(x, axis=-1, eps=1e-05):
    m = jnp.mean(x, axis=axis, keepdims=True)
    v = jnp.var(x, axis=axis, keepdims=True)
    return (x - m) / jnp.sqrt(v + eps)

def _scatter_add(tgt, idx, src, axis=0):
    return tgt.at[idx].add(src)

def _segment_sum(src, seg, n):
    return jax.ops.segment_sum(src, seg, n)
kernel_name = 'mk_rec_standalone_d1_rec_r8_16dac0'

def setup_inputs(seed: int=0):
    np.random.seed(seed)
    _w = jnp.asarray

    def _rec_inputs():
        import jax
        import jax.numpy as jnp
        _rk = jax.random.key(seed)
        r_keys = 2.81802e-05 + 1.00001 * jax.random.normal(jax.random.fold_in(_rk, 1), (512, 1024, 64), jnp.float32)
        r_queries = -0.0142567 + 1.00875 * jax.random.normal(jax.random.fold_in(_rk, 2), (512, 64), jnp.float32)
        return (r_keys, r_queries)
    r_keys, r_queries = _rec_inputs()

    def _L0_rec_setup():
        import jax, jax.numpy as jnp
        import numpy as np
        U = 64

        def _gru(keys, Wx, Wh, b_in, b_rec):
            B = keys.shape[0]
            xp = jnp.einsum('bte,eu->btu', keys, Wx) + b_in
            xp = jnp.transpose(xp, (1, 0, 2))
            h0 = jnp.zeros((B, U), keys.dtype)

            def step(h, x):
                rec = h @ Wh + b_rec
                xz, xr, xh = jnp.split(x, 3, axis=-1)
                rz, rr, rh = jnp.split(rec, 3, axis=-1)
                z = jax.nn.sigmoid(xz + rz)
                r = jax.nn.sigmoid(xr + rr)
                hh = jax.nn.relu(xh + r * rh)
                h_new = z * h + (1.0 - z) * hh
                return (h_new, h_new)
            _, outs = jax.lax.scan(step, h0, xp)
            return outs

        def _agru(outputs_tbu, attn_tb, Wx, Wh, b):
            B = outputs_tbu.shape[1]
            xp = jnp.einsum('tbu,uv->tbv', outputs_tbu, Wx) + b
            h0 = jnp.zeros((B, U), outputs_tbu.dtype)

            def step(h, inp):
                x, a = inp
                rec = h @ Wh
                xr, xc = jnp.split(x, 2, axis=-1)
                rr, rc = jnp.split(rec, 2, axis=-1)
                r = jax.nn.sigmoid(xr + rr)
                c = jax.nn.relu(xc + r * rc)
                a = a[:, None]
                h_new = (1.0 - a) * h + a * c
                return (h_new, None)
            hT, _ = jax.lax.scan(step, h0, (xp, attn_tb))
            return hT
        key = jax.random.key(seed)
        ks = jax.random.split(key, 10)
        B, T, E = (256, 1024, 64)
        s_in = (2.0 / E) ** 0.5
        s_rec = (2.0 / U) ** 0.5
        return {'queries': jax.random.normal(ks[0], (B, U), jnp.float32), 'keys': jax.random.normal(ks[1], (B, T, E), jnp.float32), 'W_att': jax.random.normal(ks[2], (U, U), jnp.float32) * s_rec, 'gru_Wx': jax.random.normal(ks[3], (E, 3 * U), jnp.float32) * s_in, 'gru_Wh': jax.random.normal(ks[4], (U, 3 * U), jnp.float32) * s_rec, 'gru_b_in': jnp.zeros((3 * U,), jnp.float32), 'gru_b_rec': jnp.zeros((3 * U,), jnp.float32), 'agru_Wx': jax.random.normal(ks[5], (U, 2 * U), jnp.float32) * s_rec, 'agru_Wh': jax.random.normal(ks[6], (U, 2 * U), jnp.float32) * s_rec, 'agru_b': jnp.zeros((2 * U,), jnp.float32)}
    _L0_rec_all = _L0_rec_setup()
    _L0_rec_in = {k: v for k, v in _L0_rec_all.items() if k in ('W_att', 'gru_Wx', 'gru_Wh', 'gru_b_in', 'gru_b_rec', 'agru_Wx', 'agru_Wh', 'agru_b')}
    del _L0_rec_all
    return {'r_keys': r_keys, 'r_queries': r_queries, 'L0_rec_W_att': _L0_rec_in['W_att'], 'L0_rec_gru_Wx': _L0_rec_in['gru_Wx'], 'L0_rec_gru_Wh': _L0_rec_in['gru_Wh'], 'L0_rec_gru_b_in': _L0_rec_in['gru_b_in'], 'L0_rec_gru_b_rec': _L0_rec_in['gru_b_rec'], 'L0_rec_agru_Wx': _L0_rec_in['agru_Wx'], 'L0_rec_agru_Wh': _L0_rec_in['agru_Wh'], 'L0_rec_agru_b': _L0_rec_in['agru_b']}

def reference(r_keys, r_queries, L0_rec_W_att, L0_rec_gru_Wx, L0_rec_gru_Wh, L0_rec_gru_b_in, L0_rec_gru_b_rec, L0_rec_agru_Wx, L0_rec_agru_Wh, L0_rec_agru_b):
    import jax
    import jax.numpy as jnp

    def _L0_rec_ref(queries, keys, W_att, gru_Wx, gru_Wh, gru_b_in, gru_b_rec, agru_Wx, agru_Wh, agru_b):
        import jax, jax.numpy as jnp
        import numpy as np
        U = 64

        def _gru(keys, Wx, Wh, b_in, b_rec):
            B = keys.shape[0]
            xp = jnp.einsum('bte,eu->btu', keys, Wx) + b_in
            xp = jnp.transpose(xp, (1, 0, 2))
            h0 = jnp.zeros((B, U), keys.dtype)

            def step(h, x):
                rec = h @ Wh + b_rec
                xz, xr, xh = jnp.split(x, 3, axis=-1)
                rz, rr, rh = jnp.split(rec, 3, axis=-1)
                z = jax.nn.sigmoid(xz + rz)
                r = jax.nn.sigmoid(xr + rr)
                hh = jax.nn.relu(xh + r * rh)
                h_new = z * h + (1.0 - z) * hh
                return (h_new, h_new)
            _, outs = jax.lax.scan(step, h0, xp)
            return outs

        def _agru(outputs_tbu, attn_tb, Wx, Wh, b):
            B = outputs_tbu.shape[1]
            xp = jnp.einsum('tbu,uv->tbv', outputs_tbu, Wx) + b
            h0 = jnp.zeros((B, U), outputs_tbu.dtype)

            def step(h, inp):
                x, a = inp
                rec = h @ Wh
                xr, xc = jnp.split(x, 2, axis=-1)
                rr, rc = jnp.split(rec, 2, axis=-1)
                r = jax.nn.sigmoid(xr + rr)
                c = jax.nn.relu(xc + r * rc)
                a = a[:, None]
                h_new = (1.0 - a) * h + a * c
                return (h_new, None)
            hT, _ = jax.lax.scan(step, h0, (xp, attn_tb))
            return hT
        outs = _gru(keys, gru_Wx, gru_Wh, gru_b_in, gru_b_rec)
        qw = queries @ W_att.T
        logit = jnp.einsum('tbu,bu->bt', outs, qw)
        attn = jax.nn.softmax(logit, axis=-1)
        final = _agru(outs, attn.T, agru_Wx, agru_Wh, agru_b)
        return final
    y = _L0_rec_ref(r_queries, r_keys, L0_rec_W_att, L0_rec_gru_Wx, L0_rec_gru_Wh, L0_rec_gru_b_in, L0_rec_gru_b_rec, L0_rec_agru_Wx, L0_rec_agru_Wh, L0_rec_agru_b)
    return y

_drawn_inputs = setup_inputs


def setup_inputs(seed=0):
    import zlib

    import numpy as np

    out = dict(_drawn_inputs(seed))
    spreads = {'L0_rec_gru_b_in': (0.0, 0.1), 'L0_rec_gru_b_rec': (0.0, 0.1), 'L0_rec_agru_b': (0.0, 0.1)}
    factors = {}
    for name, (base, spread) in spreads.items():
        noise = np.random.default_rng([zlib.crc32(name.encode()), seed]).standard_normal(out[name].shape)
        drawn = base * np.exp(spread * noise) if base else spread * noise
        out[name] = jnp.asarray(drawn.astype(out[name].dtype))
    for name, factor in factors.items():
        out[name] = (out[name] * factor).astype(out[name].dtype)
    return out
```

```python
from contextlib import ExitStack

import concourse.bass as bass
from concourse import mybir

F32 = mybir.dt.float32
ALU = mybir.AluOpType
ACT = mybir.ActivationFunctionType
AX_X = mybir.AxisListType.X

P = 128
CHUNK = 8
BODY = 2 * CHUNK
TILES = 4


def recurrent_attention_kernel(nc, keys_t, queries_t, w_att_t, gru_wx, gru_wh, gru_b_in, gru_b_rec,
                               agru_wx, agru_wh, agru_b, out):
    n_chunks, _, chunk_cols = keys_t.shape
    U = gru_wh.shape[0]
    COLS = chunk_cols // CHUNK
    T = n_chunks * CHUNK
    GC = COLS // 2
    GROUPS = (0, 1)
    HALVES = P // U
    TM = T // P
    BM = HALVES * COLS // P
    assert HALVES == 2 and GC == P and T % BODY == 0

    BODIES = T // BODY
    outs_dram = nc.dram_tensor("gru_outputs", (BODIES, 2, P, CHUNK, COLS), F32).ap()
    logits_dram = nc.dram_tensor("logits", (T + 1, HALVES, COLS), F32).ap()
    attn_dram = nc.dram_tensor("attention", (HALVES, T, COLS), F32).ap()
    keys = keys_t.rearrange("(k b) p (s c) -> k b p s c", b=2, s=CHUNK)
    attn_bodies = attn_dram.rearrange("h (k b s) c -> k b h s c", b=2, s=CHUNK)
    logit_bodies = logits_dram[0:T].rearrange("(k i j) h c -> k j i h c", j=TILES, i=BODY // TILES)

    with ExitStack() as ctx:
        def sb(name, shape):
            return ctx.enter_context(nc.sbuf_tensor(name, shape, F32))

        def bank(name):
            return ctx.enter_context(nc.psum_tensor(name, [P, 512], F32))

        def sem(name):
            return ctx.enter_context(nc.semaphore(name))

        def sems(name):
            return [sem(f"{name}_{'ab'[g]}") for g in GROUPS]

        weights = sb("weights", [P, 11, P])
        GX_Z, GX_R, GX_H, GH_Z, GH_R, GH_H, AX_R, AX_C, AH_R, AH_C, ATT = range(11)
        biases = sb("biases", [P, 8])
        BI, BR, BA = 0, 3, 6
        gate_bias = sb("gate_bias", [P, 3])
        q_t = sb("q_t", [P, COLS])
        qw = sb("qw", [P, COLS])
        ident = sb("ident", [P, P])
        row_sum = sb("row_sum", [P, BODY // TILES, 32])
        x = sb("x", [P, 2, CHUNK, COLS])
        h = sb("h", [P, 2, CHUNK, COLS])
        r_gate = sb("r_gate", [P, 2, GC])
        z_gate = sb("z_gate", [P, 2, GC])
        z_rest = sb("z_rest", [P, 2, GC])
        gated = sb("gated", [P, 2, GC])
        kept = sb("kept", [P, 2, GC])
        prod = sb("prod", [P, BODY, COLS])
        logit_rows = sb("logit_rows", [P, COLS])
        time_rows = sb("time_rows", [P, TM, HALVES * COLS])
        batch_rows = sb("batch_rows", [P, BM, T])
        softmax_stat = sb("softmax_stat", [P, 4, BM])
        attn = sb("attn", [P, 2, CHUNK, COLS])
        attn_rest = sb("attn_rest", [P, 2, COLS])
        state = sb("state", [P, 2, COLS])

        r_bank = [bank(f"r_bank_{'ab'[g]}") for g in GROUPS]
        z_bank = [bank(f"z_bank_{'ab'[g]}") for g in GROUPS]
        c_bank = [bank(f"c_bank_{'ab'[g]}") for g in GROUPS]
        logit_bank = bank("logit_bank")
        vec_bank = bank("vec_bank")

        w_zeroed, w_loaded, x_ready = sem("w_zeroed"), sem("w_loaded"), sem("const_ready")
        qw_summed, qw_ready, bias_ready = sem("qw_summed"), sem("qw_ready"), sem("bias_ready")
        id_zeroed, id_ready, sel_zeroed = sem("id_zeroed"), sem("id_ready"), sem("sel_zeroed")
        x_loaded = [sem("x_loaded_0"), sem("x_loaded_1")]
        x_used = sem("x_used")
        h_ready, r_summed, rh_summed, z_summed = sems("h_ready"), sems("r_summed"), sems("rh_summed"), sems("z_summed")
        r_ready, z_ready, zr_ready = sems("r_ready"), sems("z_ready"), sems("z_rest_ready")
        gated_ready, cand_ready, new_ready = sems("gated_ready"), sems("cand_ready"), sems("new_ready")
        kept_ready, prod_ready = sems("kept_ready"), sems("prod_ready")
        outs_stored = [sem("outs_stored_0"), sem("outs_stored_1")]
        logits_summed, logits_copied, logits_stored = sem("logits_summed"), sem("logits_copied"), sem("logits_stored")
        rows_loaded, turned, turned_copied = sem("rows_loaded"), sem("turned"), sem("turned_copied")
        stat_ready, exp_ready, probs_ready = sem("stat_ready"), sem("exp_ready"), sem("probs_ready")
        back, back_copied, attn_stored = sem("back"), sem("back_copied"), sem("attn_stored")
        a_loaded = [sem("a_loaded_0"), sem("a_loaded_1")]
        a_used = sems("a_used")
        s_ready, ar_summed, rc_summed = sems("s_ready"), sems("ar_summed"), sems("rc_summed")
        ar_ready, rest_ready = sems("ar_ready"), sem("rest_ready")
        agated_ready, acand_ready, anew_ready, akept_ready = (sems("agated_ready"), sems("acand_ready"),
                                                              sems("anew_ready"), sems("akept_ready"))
        out_stored, table_loaded = sem("out_stored"), sem("table_loaded")

        def gcols(g):
            return slice(g * GC, (g + 1) * GC)

        def h_at(s):
            s = s % BODY
            return h[:, s // CHUNK, s % CHUNK, :]

        def x_at(s):
            return x[:, s // CHUNK, s % CHUNK, :]

        def attn_at(s):
            return attn[:, s // CHUNK, s % CHUNK, :]

        N_WEIGHT_DMAS = 2 * 5 + 2 * 3 + 1
        N_TURN = TM * BM
        PER_COPY = 4
        N_COPY = N_TURN // PER_COPY

        block = ctx.enter_context(nc.Block())

        @block.sync
        def _(sp):
            sp.wait_ge(w_zeroed, 1)
            for half in range(HALVES):
                rows = slice(half * U, (half + 1) * U)
                for first, w in ((GX_Z, gru_wx), (GH_Z, gru_wh), (AX_R, agru_wx), (AH_R, agru_wh), (ATT, w_att_t)):
                    n = w.shape[1] // U
                    sp.dma_start(weights[rows, first:first + n, rows],
                                 w.rearrange("k (n u) -> k n u", n=n)).then_inc(w_loaded, 16)
                for first, b in ((BI, gru_b_in), (BR, gru_b_rec), (BA, agru_b)):
                    sp.dma_start(biases[rows, first:first + b.shape[1]], b).then_inc(w_loaded, 16)
            sp.dma_start(q_t[:], queries_t).then_inc(w_loaded, 16)

            def chunk_of(dram, k, b):
                return dram[k, b] if isinstance(k, int) else dram[bass.ds(k, 1), b].rearrange("a p s c -> (a p) s c")

            def load_x(dram, k, b):
                sp.dma_start(x[:, b], chunk_of(dram, k, b)).then_inc(x_loaded[b], 16)

            def store_outs(k, b):
                for g in GROUPS:
                    sp.wait_ge(h_ready[g], k * BODY + (CHUNK * (b + 1) + 1))
                sp.dma_start(chunk_of(outs_dram, k, b), h[:, b]).then_inc(outs_stored[b], 16)

            def store_logits(k):
                sp.wait_ge(logits_copied, k * BODY + 2 * BODY)
                for j in range(TILES):
                    dst = (logit_bodies[k, j] if isinstance(k, int)
                           else logit_bodies[bass.ds(k, 1), j].rearrange("a i h c -> (a i) h c"))
                    sp.dma_start(dst, logit_rows[32 * j:32 * j + 2 * BODY // TILES, :]).then_inc(logits_stored, 16)

            def load_attn(k, b):
                for half in range(HALVES):
                    src = (attn_bodies[k, b, half].rearrange("(a s) c -> a s c", a=1) if isinstance(k, int)
                           else attn_bodies[bass.ds(k, 1), b, half])
                    sp.dma_start(attn[half * U:(half + 1) * U, b],
                                 src.broadcast_to((U, CHUNK, COLS))).then_inc(a_loaded[b], 16)

            for b in range(2):
                sp.sem_inc(outs_stored[b], 16)
            sp.sem_inc(logits_stored, 16 * TILES)
            for b in range(2):
                load_x(keys, 0, b)
            with sp.Fori(0, BODIES - 1) as k:
                for b in range(2):
                    sp.wait_ge(x_used, k * BODY + CHUNK * (b + 1))
                    load_x(keys, k + 1, b)
                    store_outs(k, b)
                store_logits(k)
            for b in range(2):
                store_outs(BODIES - 1, b)
            store_logits(BODIES - 1)
            sp.wait_ge(logits_copied, T + BODY + 1)
            sp.dma_start(logits_dram[T], logit_rows[0:HALVES, :]).then_inc(logits_stored, 16)

            sp.wait_ge(logits_stored, 16 * (TILES * (BODIES + 1) + 1))
            for half in range(HALVES):
                sp.dma_start(time_rows[:, :, half * COLS:(half + 1) * COLS],
                             logits_dram[1:T + 1, half].rearrange("(m p) c -> p m c", p=P)).then_inc(rows_loaded, 16)
            for b in range(2):
                sp.wait_ge(outs_stored[b], 16 * (BODIES + 1))
            sp.wait_ge(x_used, T)
            for b in range(2):
                load_x(outs_dram, 0, b)
            sp.wait_ge(back_copied, N_COPY)
            for half in range(HALVES):
                sp.dma_start(attn_dram[half].rearrange("(m p) c -> p m c", p=P),
                             time_rows[:, :, half * COLS:(half + 1) * COLS]).then_inc(attn_stored, 16)
            sp.wait_ge(attn_stored, 16 * HALVES)

            for b in range(2):
                load_attn(0, b)
            with sp.Fori(0, BODIES - 1) as k:
                for b in range(2):
                    sp.wait_ge(x_used, k * BODY + (T + CHUNK * (b + 1)))
                    load_x(outs_dram, k + 1, b)
                    for g in GROUPS:
                        sp.wait_ge(anew_ready[g], k * BODY + (CHUNK * (b + 1) + 1))
                    sp.wait_ge(rest_ready, k * BODY + (CHUNK * (b + 1) + 1))
                    load_attn(k + 1, b)
            for g in GROUPS:
                sp.wait_ge(s_ready[g], T + 1)
            sp.dma_start(out, state[:, (T - 1) % 2, :]).then_inc(out_stored, 16)
            sp.wait_ge(out_stored, 16)

        @block.gpsimd
        def _(pool):
            nc.gpsimd.memset(ident[:], 0.0).then_inc(id_zeroed, 1)
            pool.wait_ge(id_zeroed, 1)
            nc.gpsimd.affine_select(out=ident[:], in_=ident[:], compare_op=ALU.not_equal, fill=1.0, base=0,
                                    pattern=[[-1, P]], channel_multiplier=1).then_inc(id_ready, 1)
            for g in GROUPS:
                pool.sem_inc(kept_ready[g], 1)
                pool.sem_inc(prod_ready[g], 1)
                pool.sem_inc(akept_ready[g], 1)
            pool.wait_ge(qw_ready, 1)

            def product(s, g):
                nc.gpsimd.tensor_tensor(prod[:, s, gcols(g)], h_at(s - 1)[:, gcols(g)], qw[:, gcols(g)],
                                        ALU.mult).then_inc(prod_ready[g], 1)

            with pool.Fori(0, T, BODY) as t0:
                for s in range(BODY):
                    for g in GROUPS:
                        pool.wait_ge(z_ready[g], t0 + (s + 2))
                        nc.gpsimd.tensor_tensor(kept[:, g], z_gate[:, g], h_at(s - 1)[:, gcols(g)],
                                                ALU.mult).then_inc(kept_ready[g], 1)
                        if g == 0 and s % TILES == 0:
                            pool.wait_ge(logits_summed, t0 + (s + TILES))
                        product(s, g)
            pool.wait_ge(logits_summed, T + TILES)
            for g in GROUPS:
                pool.wait_ge(h_ready[g], T + 1)
                product(0, g)

            with pool.Fori(0, T, BODY) as t0:
                for s in range(BODY):
                    for g in GROUPS:
                        if g == 0:
                            pool.wait_ge(rest_ready, t0 + (s + 2))
                        pool.wait_ge(s_ready[g], t0 + (s + 1))
                        nc.gpsimd.tensor_tensor(kept[:, g], attn_rest[:, s % 2, gcols(g)],
                                                state[:, (s - 1) % 2, gcols(g)], ALU.mult).then_inc(akept_ready[g], 1)

        @block.scalar
        def _(act):
            for g in GROUPS:
                for q in (r_ready[g], z_ready[g], zr_ready[g], ar_ready[g]):
                    act.sem_inc(q, 1)
            act.sem_inc(rest_ready, 1)
            act.sem_inc(logits_copied, BODY)
            act.wait_ge(bias_ready, 2)
            nc.scalar.activation(r_gate[:, 0, 0:1], gate_bias[:, 0:1], ACT.Sigmoid).then_inc(table_loaded, 1)
            act.wait_ge(table_loaded, 1)
            with act.Fori(0, T, BODY) as t0:
                for s in range(BODY):
                    for g in GROUPS:
                        act.wait_ge(r_summed[g], t0 + (s + 2))
                        nc.scalar.activation(r_gate[:, g], r_bank[g][:, 0:GC], ACT.Sigmoid,
                                             bias=gate_bias[:, 1:2]).then_inc(r_ready[g], 1)
                        act.wait_ge(z_summed[g], t0 + (s + 2))
                        nc.scalar.activation(z_gate[:, g], z_bank[g][:, 0:GC], ACT.Sigmoid,
                                             bias=gate_bias[:, 0:1]).then_inc(z_ready[g], 1)
                        nc.scalar.activation(z_rest[:, g], z_bank[g][:, 0:GC], ACT.Sigmoid, scale=-1.0,
                                             bias=gate_bias[:, 2:3]).then_inc(zr_ready[g], 1)
                act.wait_ge(logits_summed, t0 + 2 * BODY)
                act.wait_ge(logits_stored, t0 * TILES + 16 * TILES)
                nc.scalar.activation(logit_rows[:], logit_bank[:, 0:COLS], ACT.Copy).then_inc(logits_copied, BODY)
            act.wait_ge(logits_summed, T + BODY + 1)
            act.wait_ge(logits_stored, 16 * TILES * (T // BODY + 1))
            nc.scalar.activation(logit_rows[0:32], logit_bank[0:32, 0:COLS], ACT.Copy).then_inc(logits_copied, 1)

            act.wait_ge(stat_ready, BM + 1)
            for m in range(BM):
                nc.scalar.activation(batch_rows[:, m], batch_rows[:, m], ACT.Exp, bias=softmax_stat[:, 1, m:m + 1],
                                     accum_out=softmax_stat[:, 2, m:m + 1]).then_inc(exp_ready, 1)
            nc.scalar.activation(r_gate[:, 0, 0:1], gate_bias[:, 0:1], ACT.Sigmoid).then_inc(table_loaded, 1)
            act.wait_ge(table_loaded, 2)

            with act.Fori(0, T, BODY) as t0:
                for s in range(BODY):
                    if s % CHUNK == 0:
                        act.wait_ge(a_loaded[s // CHUNK], t0 * 2 + 32)
                    for g in GROUPS:
                        if s >= 2:
                            act.wait_ge(akept_ready[g], t0 + (s + 0))
                    nc.scalar.activation(attn_rest[:, s % 2], attn_at(s), ACT.Copy, bias=1.0,
                                         scale=-1.0).then_inc(rest_ready, 1)
                    for g in GROUPS:
                        act.wait_ge(ar_summed[g], t0 + (s + 2))
                        nc.scalar.activation(r_gate[:, g], r_bank[g][:, 0:GC], ACT.Sigmoid,
                                             bias=biases[:, BA:BA + 1]).then_inc(ar_ready[g], 1)

        @block.vector
        def _(dve):
            nc.vector.memset(weights[:], 0.0).then_inc(w_zeroed, 1)
            nc.vector.memset(row_sum[:], 0.0).then_inc(sel_zeroed, 1)
            dve.wait_ge(sel_zeroed, 1)
            for k in range(BODY // TILES):
                for half in range(HALVES):
                    nc.vector.memset(row_sum[half * U:(half + 1) * U, k, 2 * k + half:2 * k + half + 1],
                                     1.0).then_inc(x_ready, 1)
            dve.wait_ge(w_loaded, 16 * N_WEIGHT_DMAS)
            nc.vector.tensor_tensor(gate_bias[:, 0:2], biases[:, BI:BI + 2], biases[:, BR:BR + 2], ALU.add).then_inc(bias_ready, 1)
            dve.wait_ge(bias_ready, 1)
            nc.vector.tensor_scalar(gate_bias[:, 2:3], gate_bias[:, 0:1], -1.0, None, ALU.mult).then_inc(bias_ready, 1)
            dve.wait_ge(qw_summed, 1)
            nc.vector.tensor_copy(qw[:], logit_bank[:, 0:COLS]).then_inc(qw_ready, 1)
            for g in GROUPS:
                for q in (gated_ready[g], cand_ready[g], new_ready[g], agated_ready[g], acand_ready[g], anew_ready[g]):
                    dve.sem_inc(q, 1)
            for g in GROUPS:
                nc.vector.memset(h_at(-1)[:, gcols(g)], 0.0).then_inc(h_ready[g], 1)
                nc.vector.memset(state[:, 1, gcols(g)], 0.0).then_inc(s_ready[g], 1)

            with dve.Fori(0, T, BODY) as t0:
                for s in range(BODY):
                    for g in GROUPS:
                        hid, inp = c_bank[g][:, 0:GC], c_bank[g][:, GC:2 * GC]
                        cand, new = vec_bank[:, g * GC:(g + 1) * GC], vec_bank[:, (2 + g) * GC:(3 + g) * GC]
                        dve.wait_ge(rh_summed[g], t0 + (s + 2))
                        dve.wait_ge(r_ready[g], t0 + (s + 2))
                        nc.vector.scalar_tensor_tensor(gated[:, g], hid, biases[:, BR + 2:BR + 3], r_gate[:, g],
                                                       ALU.add, ALU.mult).then_inc(gated_ready[g], 1)
                        dve.wait_ge(gated_ready[g], t0 + (s + 2))
                        nc.vector.scalar_tensor_tensor(cand, inp, biases[:, BI + 2:BI + 3], gated[:, g],
                                                       ALU.add, ALU.add).then_inc(cand_ready[g], 1)
                        dve.wait_ge(cand_ready[g], t0 + (s + 2))
                        dve.wait_ge(zr_ready[g], t0 + (s + 2))
                        nc.vector.scalar_tensor_tensor(new, cand, 0.0, z_rest[:, g],
                                                       ALU.max, ALU.mult).then_inc(new_ready[g], 1)
                        if s % CHUNK == 0:
                            dve.wait_ge(outs_stored[s // CHUNK], t0 + 16)
                        dve.wait_ge(new_ready[g], t0 + (s + 2))
                        dve.wait_ge(kept_ready[g], t0 + (s + 2))
                        nc.vector.tensor_tensor(h_at(s)[:, gcols(g)], new, kept[:, g], ALU.add).then_inc(h_ready[g], 1)

            for n in range(N_COPY):
                dve.wait_ge(turned, n + 1)
                m, part = n // (TM // PER_COPY), n % (TM // PER_COPY)
                src = (r_bank + z_bank)[n % 4]
                nc.vector.tensor_copy(batch_rows[:, m, part * 512:(part + 1) * 512], src[:]).then_inc(turned_copied, 1)
            dve.wait_ge(turned_copied, N_COPY)
            for m in range(BM):
                nc.vector.reduce_max(softmax_stat[:, 0, m:m + 1], batch_rows[:, m], AX_X).then_inc(stat_ready, 1)
            dve.wait_ge(stat_ready, BM)
            nc.vector.tensor_scalar(softmax_stat[:, 1], softmax_stat[:, 0], -1.0, None, ALU.mult).then_inc(stat_ready, 1)
            dve.wait_ge(exp_ready, BM)
            nc.vector.reciprocal(softmax_stat[:, 3], softmax_stat[:, 2]).then_inc(stat_ready, 1)
            dve.wait_ge(stat_ready, BM + 2)
            for m in range(BM):
                nc.vector.tensor_scalar(batch_rows[:, m], batch_rows[:, m], softmax_stat[:, 3, m:m + 1], None,
                                        ALU.mult).then_inc(probs_ready, 1)
            for n in range(N_COPY):
                dve.wait_ge(back, n + 1)
                nc.vector.tensor_copy(time_rows[:, n, :], (r_bank + z_bank)[n % 4][:]).then_inc(back_copied, 1)

            with dve.Fori(0, T, BODY) as t0:
                for s in range(BODY):
                    for g in GROUPS:
                        hid, inp = c_bank[g][:, 0:GC], c_bank[g][:, GC:2 * GC]
                        cand, new = vec_bank[:, g * GC:(g + 1) * GC], vec_bank[:, (2 + g) * GC:(3 + g) * GC]
                        dve.wait_ge(rc_summed[g], t0 + (s + 2))
                        dve.wait_ge(ar_ready[g], t0 + (s + 2))
                        nc.vector.tensor_tensor(gated[:, g], hid, r_gate[:, g], ALU.mult).then_inc(agated_ready[g], 1)
                        dve.wait_ge(agated_ready[g], t0 + (s + 2))
                        nc.vector.scalar_tensor_tensor(cand, inp, biases[:, BA + 1:BA + 2], gated[:, g],
                                                       ALU.add, ALU.add).then_inc(acand_ready[g], 1)
                        if g == 0 and s % CHUNK == 0:
                            dve.wait_ge(a_loaded[s // CHUNK], t0 * 2 + 32)
                        dve.wait_ge(acand_ready[g], t0 + (s + 2))
                        nc.vector.scalar_tensor_tensor(new, cand, 0.0, attn_at(s)[:, gcols(g)],
                                                       ALU.max, ALU.mult).then_inc(anew_ready[g], 1)
                        dve.wait_ge(anew_ready[g], t0 + (s + 2))
                        dve.wait_ge(akept_ready[g], t0 + (s + 2))
                        nc.vector.tensor_tensor(state[:, s % 2, gcols(g)], new, kept[:, g], ALU.add).then_inc(s_ready[g], 1)

        @block.tensor
        def _(pe):
            pe.wait_ge(w_loaded, 16 * N_WEIGHT_DMAS)
            nc.tensor.matmul(logit_bank[:, 0:COLS], weights[:, ATT], q_t[:], start=True, stop=True).then_inc(qw_summed, 1)
            for g in GROUPS:
                for q in (r_summed[g], rh_summed[g], z_summed[g], ar_summed[g], rc_summed[g]):
                    pe.sem_inc(q, 1)
            pe.wait_ge(qw_ready, 1)
            pe.sem_inc(logits_summed, BODY)
            pe.wait_ge(x_ready, 2 * BODY // TILES)

            def mm(dst, w, moving, start, stop):
                return nc.tensor.matmul(dst, weights[:, w], moving, start=start, stop=stop, skip_group_check=True)

            def logit(s, last):
                j, k = s % TILES, s // TILES
                return nc.tensor.matmul(logit_bank[32 * j:32 * (j + 1), 0:COLS], row_sum[:, k], prod[:, s],
                                        start=(k == 0), stop=last, skip_group_check=True)

            with pe.Fori(0, T, BODY) as t0:
                for s in range(BODY):
                    if s > 4 and s % TILES == 1:
                        for g in GROUPS:
                            pe.wait_ge(prod_ready[g], t0 + (s - 1 + 1))
                        if s == 5:
                            pe.wait_ge(logits_copied, t0 + BODY)
                        for k in range(TILES):
                            last = logit(s - 1 - TILES + k, False)
                        last.then_inc(logits_summed, TILES)
                    for g in GROUPS:
                        xs, hs = x_at(s)[:, gcols(g)], h_at(s - 1)[:, gcols(g)]
                        if g == 0 and s % CHUNK == 0:
                            pe.wait_ge(x_loaded[s // CHUNK], t0 + 16)
                        pe.wait_ge(r_ready[g], t0 + (s + 1))
                        mm(r_bank[g][:, 0:GC], GX_R, xs, True, False)
                        pe.wait_ge(zr_ready[g], t0 + (s + 1))
                        mm(z_bank[g][:, 0:GC], GX_Z, xs, True, False)
                        pe.wait_ge(cand_ready[g], t0 + (s + 1))
                        last = mm(c_bank[g][:, GC:2 * GC], GX_H, xs, True, False)
                        if g == 1 and s % CHUNK == CHUNK - 1:
                            last.then_inc(x_used, CHUNK)
                        pe.wait_ge(h_ready[g], t0 + (s + 1))
                        mm(r_bank[g][:, 0:GC], GH_R, hs, False, True).then_inc(r_summed[g], 1)
                        mm(c_bank[g][:, 0:GC], GH_H, hs, False, True).then_inc(rh_summed[g], 1)
                        mm(z_bank[g][:, 0:GC], GH_Z, hs, False, True).then_inc(z_summed[g], 1)
                for g in GROUPS:
                    pe.wait_ge(prod_ready[g], t0 + (BODY + 1))
                for k in range(TILES):
                    last = logit(BODY - TILES + k, True)
                last.then_inc(logits_summed, TILES)
            for g in GROUPS:
                pe.wait_ge(prod_ready[g], T + 2)
            pe.wait_ge(logits_copied, T + BODY)
            logit(0, True).then_inc(logits_summed, 1)

            pe.wait_ge(id_ready, 1)
            pe.wait_ge(rows_loaded, 16 * HALVES)
            for n in range(N_COPY):
                if n == 0:
                    for g in GROUPS:
                        pe.wait_ge(zr_ready[g], T + 1)
                if n >= 4:
                    pe.wait_ge(turned_copied, n - 3)
                dst = (r_bank + z_bank)[n % 4]
                for k in range(PER_COPY):
                    m, tm = n // (TM // PER_COPY), n % (TM // PER_COPY) * PER_COPY + k
                    last = nc.tensor.transpose(dst[:, k * P:(k + 1) * P], time_rows[:, tm, m * P:(m + 1) * P], ident[:])
                last.then_inc(turned, 1)
            for n in range(N_COPY):
                if n == 0:
                    pe.wait_ge(probs_ready, BM)
                if n >= 4:
                    pe.wait_ge(back_copied, n - 3)
                dst = (r_bank + z_bank)[n % 4]
                for m in range(BM):
                    last = nc.tensor.transpose(dst[:, m * P:(m + 1) * P], batch_rows[:, m, n * P:(n + 1) * P], ident[:])
                last.then_inc(back, 1)
            pe.wait_ge(back_copied, N_COPY)

            with pe.Fori(0, T, BODY) as t0:
                for s in range(BODY):
                    for g in GROUPS:
                        xs, hs = x_at(s)[:, gcols(g)], state[:, (s - 1) % 2, gcols(g)]
                        if g == 0 and s % CHUNK == 0:
                            pe.wait_ge(x_loaded[s // CHUNK], t0 + (T + 16))
                        pe.wait_ge(ar_ready[g], t0 + (s + 1))
                        mm(r_bank[g][:, 0:GC], AX_R, xs, True, False)
                        pe.wait_ge(acand_ready[g], t0 + (s + 1))
                        last = mm(c_bank[g][:, GC:2 * GC], AX_C, xs, True, False)
                        if g == 1 and s % CHUNK == CHUNK - 1:
                            last.then_inc(x_used, CHUNK)
                        pe.wait_ge(s_ready[g], t0 + (s + 1))
                        mm(r_bank[g][:, 0:GC], AH_R, hs, False, True).then_inc(ar_summed[g], 1)
                        mm(c_bank[g][:, 0:GC], AH_C, hs, False, True).then_inc(rc_summed[g], 1)


def kernel(r_keys, r_queries, L0_rec_W_att, L0_rec_gru_Wx, L0_rec_gru_Wh, L0_rec_gru_b_in, L0_rec_gru_b_rec,
           L0_rec_agru_Wx, L0_rec_agru_Wh, L0_rec_agru_b):
    import numpy as np
    import concourse.bacc as bacc
    from concourse.bass_utils import run_bass_kernel_spmd

    B, T, E = r_keys.shape
    half = B // 2
    keys = np.asarray(r_keys).reshape(2, half, T // CHUNK, CHUNK, E)
    arrays = {
        "keys_t": keys.transpose(2, 0, 4, 3, 1).reshape(T // CHUNK, 2 * E, CHUNK * half),
        "queries_t": np.asarray(r_queries).reshape(2, half, -1).transpose(0, 2, 1).reshape(-1, half),
        "w_att_t": np.asarray(L0_rec_W_att).T,
        "gru_wx": np.asarray(L0_rec_gru_Wx),
        "gru_wh": np.asarray(L0_rec_gru_Wh),
        "gru_b_in": np.asarray(L0_rec_gru_b_in).reshape(3, -1).T,
        "gru_b_rec": np.asarray(L0_rec_gru_b_rec).reshape(3, -1).T,
        "agru_wx": np.asarray(L0_rec_agru_Wx),
        "agru_wh": np.asarray(L0_rec_agru_Wh),
        "agru_b": np.asarray(L0_rec_agru_b).reshape(2, -1).T,
    }
    arrays = {k: np.ascontiguousarray(v) for k, v in arrays.items()}
    nc = bacc.Bacc("TRN2", target_bir_lowering=False, num_devices=1)
    args = [nc.dram_tensor(f"in_{k}", v.shape, F32, kind="ExternalInput").ap() for k, v in arrays.items()]
    out = nc.dram_tensor("out_state", (2 * E, half), F32, kind="ExternalOutput").ap()
    recurrent_attention_kernel(nc, *args, out)
    r = run_bass_kernel_spmd(nc, [{f"in_{k}": v for k, v in arrays.items()}], core_ids=[0])
    state = r.results[0]["out_state"]
    return np.ascontiguousarray(state.reshape(2, E, half).transpose(0, 2, 1).reshape(B, E))
```

```python
from contextlib import ExitStack

import concourse.bass as bass
from concourse import mybir

F32 = mybir.dt.float32
BF16 = mybir.dt.bfloat16
QUAD = 32
ALU = mybir.AluOpType
ACT = mybir.ActivationFunctionType
AX_X = mybir.AxisListType.X

P = 128
CHUNK = 8
BODY = 2 * CHUNK
TILES = 4


def recurrent_attention_kernel(nc, keys_t, queries_t, w_att_t, gru_wx, gru_wh, gru_b_in, gru_b_rec,
                               agru_wx, agru_wh, agru_b, agru_b_row, out):
    n_chunks, _, chunk_cols = keys_t.shape
    U = gru_wh.shape[0]
    COLS = chunk_cols // CHUNK
    T = n_chunks * CHUNK
    GC = COLS // 2
    GROUPS = (0, 1)
    HALVES = P // U
    TM = T // P
    BM = HALVES * COLS // P
    assert HALVES == 2 and GC == P and T % BODY == 0

    BODIES = T // BODY
    ROW0 = BODY + 1
    outs_dram = nc.dram_tensor("gru_outputs", (BODIES, 2, P, CHUNK, COLS), F32).ap()
    logits_dram = nc.dram_tensor("logits", (T + ROW0, HALVES, COLS), F32).ap()
    attn_dram = nc.dram_tensor("attention", (HALVES, T, COLS), F32).ap()
    keys = keys_t.rearrange("(k b) p (s c) -> k b p s c", b=2, s=CHUNK)
    attn_bodies = attn_dram.rearrange("h (k b s) c -> k b h s c", b=2, s=CHUNK)
    logit_bodies = logits_dram[0:T + BODY].rearrange("(k i j) h c -> k j i h c", j=TILES, i=BODY // TILES)

    with ExitStack() as ctx:
        def sb(name, shape):
            return ctx.enter_context(nc.sbuf_tensor(name, shape, F32))

        def bank(name):
            return ctx.enter_context(nc.psum_tensor(name, [P, 512], F32))

        def sem(name):
            return ctx.enter_context(nc.semaphore(name))

        def sems(name):
            return [sem(f"{name}_{'ab'[g]}") for g in GROUPS]

        weights = sb("weights", [P, 11, P])
        GX_Z, GX_R, GX_H, GH_Z, GH_R, GH_H, AX_R, AX_C, AH_R, AH_C, ATT = range(11)
        biases = sb("biases", [P, 8])
        BI, BR, BA = 0, 3, 6
        gate_bias = sb("gate_bias", [P, 3])
        q_t = sb("q_t", [P, COLS])
        qw = sb("qw", [P, COLS])
        ident = sb("ident", [P, P])
        bias_rows = sb("bias_rows", [P, 2, P])
        bias_part = ctx.enter_context(nc.sbuf_tensor("bias_part", [P, 3, 2, P], BF16))
        bias_left = sb("bias_left", [P, 2, 2, P])
        bias_split = ctx.enter_context(nc.sbuf_tensor("bias_split", [P, 2, P], BF16))
        ones = ctx.enter_context(nc.sbuf_tensor("ones", [P, GC], BF16))
        row_sum = sb("row_sum", [P, BODY // TILES, 32])
        x = sb("x", [P, 2, CHUNK, COLS])
        h = sb("h", [P, 2, CHUNK, COLS])
        r_gate = sb("r_gate", [P, 2, GC])
        z_gate = sb("z_gate", [P, 2, GC])
        z_rest = sb("z_rest", [P, 2, GC])
        gated = sb("gated", [P, 2, GC])
        kept = sb("kept", [P, 2, GC])
        prod = sb("prod", [P, BODY, COLS])
        logit_rows = sb("logit_rows", [P, COLS])
        time_rows = sb("time_rows", [P, TM, HALVES * COLS])
        batch_rows = sb("batch_rows", [P, BM, T])
        softmax_stat = sb("softmax_stat", [P, 4, BM])
        attn = sb("attn", [P, 2, CHUNK, COLS])
        attn_rest = sb("attn_rest", [P, 2, COLS])
        state = sb("state", [P, 2, COLS])

        r_bank = [bank(f"r_bank_{'ab'[g]}") for g in GROUPS]
        z_bank = [bank(f"z_bank_{'ab'[g]}") for g in GROUPS]
        c_bank = [bank(f"c_bank_{'ab'[g]}") for g in GROUPS]
        logit_bank = bank("logit_bank")
        vec_bank = bank("vec_bank")

        w_zeroed, w_loaded, consts_ready = sem("w_zeroed"), sem("w_loaded"), sem("consts_ready")
        qw_summed, qw_ready, bias_ready = sem("qw_summed"), sem("qw_ready"), sem("bias_ready")
        id_zeroed, id_ready, sel_zeroed = sem("id_zeroed"), sem("id_ready"), sem("sel_zeroed")
        x_loaded = [sem("x_loaded_0"), sem("x_loaded_1")]
        x_used = sem("x_used")
        h_ready, r_summed, rh_summed, z_summed = sems("h_ready"), sems("r_summed"), sems("rh_summed"), sems("z_summed")
        r_ready, z_ready, zr_ready = sems("r_ready"), sems("z_ready"), sems("z_rest_ready")
        gated_ready, cand_ready, new_ready = sems("gated_ready"), sems("cand_ready"), sems("new_ready")
        kept_ready, prod_ready = sems("kept_ready"), sems("prod_ready")
        outs_stored = [sem("outs_stored_0"), sem("outs_stored_1")]
        logits_summed, logits_copied, logits_stored = sem("logits_summed"), sem("logits_copied"), sem("logits_stored")
        rows_loaded, turned, turned_copied = sem("rows_loaded"), sem("turned"), sem("turned_copied")
        stat_ready, exp_ready, probs_ready = sem("stat_ready"), sem("exp_ready"), sem("probs_ready")
        back, back_copied = sem("back"), sem("back_copied")
        attn_stored = [sem("attn_stored_first"), sem("attn_stored_rest")]
        a_loaded = [sem("a_loaded_0"), sem("a_loaded_1")]
        a_used = sems("a_used")
        s_ready, ar_summed, rc_summed = sems("s_ready"), sems("ar_summed"), sems("rc_summed")
        ar_ready, rest_ready = sems("ar_ready"), sem("rest_ready")
        akept_ready = sems("akept_ready")
        agated_ready, acand_ready, anew_ready = (
            [[sem(f"{name}_{'ab'[g]}{part}") for part in range(2)] for g in GROUPS]
            for name in ("agated_ready", "acand_ready", "anew_ready"))
        split_done = sem("split_done")
        out_stored, table_loaded = sem("out_stored"), sem("table_loaded")

        PARTS = ((0, slice(0, GC // 2)), (1, slice(GC // 2, GC)))

        def gcols(g):
            return slice(g * GC, (g + 1) * GC)

        def h_at(s):
            s = s % BODY
            return h[:, s // CHUNK, s % CHUNK, :]

        def x_at(s):
            return x[:, s // CHUNK, s % CHUNK, :]

        def attn_at(s):
            return attn[:, s // CHUNK, s % CHUNK, :]

        N_WEIGHT_DMAS = 2 * 5 + 2 * 3 + 1 + 3
        N_TURN = TM * BM
        PER_COPY = 4
        N_COPY = N_TURN // PER_COPY

        block = ctx.enter_context(nc.Block())

        @block.sync
        def _(sp):
            sp.wait_ge(w_zeroed, 2)
            for half in range(HALVES):
                rows = slice(half * U, (half + 1) * U)
                for first, w in ((GX_Z, gru_wx), (GH_Z, gru_wh), (AX_R, agru_wx), (AH_R, agru_wh), (ATT, w_att_t)):
                    n = w.shape[1] // U
                    sp.dma_start(weights[rows, first:first + n, rows],
                                 w.rearrange("k (n u) -> k n u", n=n)).then_inc(w_loaded, 16)
                for first, b in ((BI, gru_b_in), (BR, gru_b_rec), (BA, agru_b)):
                    sp.dma_start(biases[rows, first:first + b.shape[1]], b).then_inc(w_loaded, 16)
            sp.dma_start(q_t[:], queries_t).then_inc(w_loaded, 16)
            for i in range(3):
                sp.dma_start(bias_rows[QUAD * i:QUAD * i + 1], agru_b_row).then_inc(w_loaded, 16)

            def chunk_of(dram, k, b):
                return dram[k, b] if isinstance(k, int) else dram[bass.ds(k, 1), b].rearrange("a p s c -> (a p) s c")

            def load_x(dram, k, b):
                sp.dma_start(x[:, b], chunk_of(dram, k, b)).then_inc(x_loaded[b], 16)

            def store_outs(k, b):
                for g in GROUPS:
                    sp.wait_ge(h_ready[g], k * BODY + (CHUNK * (b + 1) + 1))
                sp.dma_start(chunk_of(outs_dram, k, b), h[:, b]).then_inc(outs_stored[b], 16)

            def store_logits(k):
                sp.wait_ge(logits_copied, k * BODY + BODY)
                for j in range(TILES):
                    dst = (logit_bodies[k, j] if isinstance(k, int)
                           else logit_bodies[bass.ds(k, 1), j].rearrange("a i h c -> (a i) h c"))
                    sp.dma_start(dst, logit_rows[32 * j:32 * j + 2 * BODY // TILES, :]).then_inc(logits_stored, 16)

            def load_attn(k, b):
                for half in range(HALVES):
                    src = (attn_bodies[k, b, half].rearrange("(a s) c -> a s c", a=1) if isinstance(k, int)
                           else attn_bodies[bass.ds(k, 1), b, half])
                    sp.dma_start(attn[half * U:(half + 1) * U, b],
                                 src.broadcast_to((U, CHUNK, COLS))).then_inc(a_loaded[b], 16)

            for b in range(2):
                sp.sem_inc(outs_stored[b], 16)
            sp.sem_inc(logits_stored, 16 * TILES)
            for b in range(2):
                load_x(keys, 0, b)
            with sp.Fori(0, BODIES - 1) as k:
                for b in range(2):
                    sp.wait_ge(x_used, k * BODY + CHUNK * (b + 1))
                    load_x(keys, k + 1, b)
                    store_outs(k, b)
                store_logits(k)
            for b in range(2):
                store_outs(BODIES - 1, b)
            store_logits(BODIES - 1)
            store_logits(BODIES)
            sp.wait_ge(logits_copied, T + BODY + 1)
            sp.dma_start(logits_dram[T + BODY], logit_rows[0:HALVES, :]).then_inc(logits_stored, 16)

            sp.wait_ge(logits_stored, 16 * (TILES * (BODIES + 2) + 1))
            for half in range(HALVES):
                sp.dma_start(time_rows[:, :, half * COLS:(half + 1) * COLS],
                             logits_dram[ROW0:ROW0 + T, half].rearrange("(m p) c -> p m c", p=P)).then_inc(rows_loaded, 16)
            for b in range(2):
                sp.wait_ge(outs_stored[b], 16 * (BODIES + 1))
            sp.wait_ge(x_used, T)
            for b in range(2):
                load_x(outs_dram, 0, b)
            for m in range(TM):
                sp.wait_ge(back_copied, m + 1)
                for half in range(HALVES):
                    sp.dma_start(attn_dram[half, m * P:(m + 1) * P],
                                 time_rows[:, m, half * COLS:(half + 1) * COLS]).then_inc(attn_stored[min(m, 1)], 16)
                if m == 0:
                    sp.wait_ge(attn_stored[0], 16 * HALVES)
                    for b in range(2):
                        load_attn(0, b)
            sp.wait_ge(attn_stored[1], 16 * HALVES * (TM - 1))
            with sp.Fori(0, BODIES - 1) as k:
                for b in range(2):
                    sp.wait_ge(x_used, k * BODY + (T + CHUNK * (b + 1)))
                    load_x(outs_dram, k + 1, b)
                    for g in GROUPS:
                        sp.wait_ge(anew_ready[g][1], k * BODY + (CHUNK * (b + 1) + 1))
                    sp.wait_ge(rest_ready, k * BODY + (CHUNK * (b + 1) + 1))
                    load_attn(k + 1, b)
            for g in GROUPS:
                sp.wait_ge(s_ready[g], T + 1)
            sp.dma_start(out, state[:, (T - 1) % 2, :]).then_inc(out_stored, 16)
            sp.wait_ge(out_stored, 16)

        @block.gpsimd
        def _(pool):
            nc.gpsimd.memset(ident[:], 0.0).then_inc(id_zeroed, 1)
            pool.wait_ge(id_zeroed, 1)
            nc.gpsimd.affine_select(out=ident[:], in_=ident[:], compare_op=ALU.not_equal, fill=1.0, base=0,
                                    pattern=[[-1, P]], channel_multiplier=1).then_inc(id_ready, 1)
            for g in GROUPS:
                pool.sem_inc(kept_ready[g], 1)
                pool.sem_inc(prod_ready[g], 1)
                pool.sem_inc(akept_ready[g], 1)
            pool.wait_ge(qw_ready, 1)

            def product(s, g):
                nc.gpsimd.tensor_tensor(prod[:, s, gcols(g)], h_at(s - 1)[:, gcols(g)], qw[:, gcols(g)],
                                        ALU.mult).then_inc(prod_ready[g], 1)

            with pool.Fori(0, T, BODY) as t0:
                for s in range(BODY):
                    for g in GROUPS:
                        pool.wait_ge(z_ready[g], t0 + (s + 2))
                        nc.gpsimd.tensor_tensor(kept[:, g], z_gate[:, g], h_at(s - 1)[:, gcols(g)],
                                                ALU.mult).then_inc(kept_ready[g], 1)
                        if g == 0 and s % TILES == 0:
                            pool.wait_ge(logits_summed, t0 + (s + BODY // 2))
                        product(s, g)
            pool.wait_ge(logits_summed, T + BODY // 2)
            for g in GROUPS:
                pool.wait_ge(h_ready[g], T + 1)
                product(0, g)

            with pool.Fori(0, T, BODY) as t0:
                for s in range(BODY):
                    for g in GROUPS:
                        if g == 0:
                            pool.wait_ge(rest_ready, t0 + (s + 2))
                        pool.wait_ge(s_ready[g], t0 + (s + 1))
                        nc.gpsimd.tensor_tensor(kept[:, g], attn_rest[:, s % 2, gcols(g)],
                                                state[:, (s - 1) % 2, gcols(g)], ALU.mult).then_inc(akept_ready[g], 1)

        @block.scalar
        def _(act):
            for g in GROUPS:
                for q in (r_ready[g], z_ready[g], zr_ready[g], ar_ready[g]):
                    act.sem_inc(q, 1)
            act.sem_inc(rest_ready, 1)
            act.wait_ge(bias_ready, 2)
            nc.scalar.activation(r_gate[:, 0, 0:1], gate_bias[:, 0:1], ACT.Sigmoid).then_inc(table_loaded, 1)
            act.wait_ge(table_loaded, 1)

            def copy_logits(t0):
                act.wait_ge(logits_summed, t0 + (BODY + TILES))
                act.wait_ge(logits_stored, t0 * TILES + 16 * TILES)
                nc.scalar.activation(logit_rows[:], logit_bank[:, 0:COLS], ACT.Copy).then_inc(logits_copied, BODY)

            with act.Fori(0, T, BODY) as t0:
                for s in range(BODY):
                    for g in GROUPS:
                        act.wait_ge(r_summed[g], t0 + (s + 2))
                        nc.scalar.activation(r_gate[:, g], r_bank[g][:, 0:GC], ACT.Sigmoid,
                                             bias=gate_bias[:, 1:2]).then_inc(r_ready[g], 1)
                        act.wait_ge(z_summed[g], t0 + (s + 2))
                        nc.scalar.activation(z_gate[:, g], z_bank[g][:, 0:GC], ACT.Sigmoid,
                                             bias=gate_bias[:, 0:1]).then_inc(z_ready[g], 1)
                        nc.scalar.activation(z_rest[:, g], z_bank[g][:, 0:GC], ACT.Sigmoid, scale=-1.0,
                                             bias=gate_bias[:, 2:3]).then_inc(zr_ready[g], 1)
                    if s == 2:
                        copy_logits(t0)
            copy_logits(T)
            act.wait_ge(logits_summed, T + BODY + TILES + 1)
            act.wait_ge(logits_stored, 16 * TILES * (BODIES + 2))
            nc.scalar.activation(logit_rows[0:32], logit_bank[0:32, 0:COLS], ACT.Copy).then_inc(logits_copied, 1)

            act.wait_ge(stat_ready, BM + 1)
            for m in range(BM):
                nc.scalar.activation(batch_rows[:, m], batch_rows[:, m], ACT.Exp, bias=softmax_stat[:, 1, m:m + 1],
                                     accum_out=softmax_stat[:, 2, m:m + 1]).then_inc(exp_ready, 1)
            nc.scalar.activation(r_gate[:, 0, 0:1], gate_bias[:, 0:1], ACT.Sigmoid).then_inc(table_loaded, 1)
            act.wait_ge(table_loaded, 2)

            with act.Fori(0, T, BODY) as t0:
                for s in range(BODY):
                    if s % CHUNK == 0:
                        act.wait_ge(a_loaded[s // CHUNK], t0 * 2 + 32)
                    for g in GROUPS:
                        if s >= 2:
                            act.wait_ge(akept_ready[g], t0 + (s + 0))
                    nc.scalar.activation(attn_rest[:, s % 2], attn_at(s), ACT.Copy, bias=1.0,
                                         scale=-1.0).then_inc(rest_ready, 1)
                    for g in GROUPS:
                        act.wait_ge(ar_summed[g], t0 + (s + 2))
                        nc.scalar.activation(r_gate[:, g], r_bank[g][:, 0:GC], ACT.Sigmoid).then_inc(ar_ready[g], 1)

        @block.vector
        def _(dve):
            nc.vector.memset(weights[:], 0.0).then_inc(w_zeroed, 1)
            nc.vector.memset(bias_rows[:], 0.0).then_inc(w_zeroed, 1)
            nc.vector.memset(bias_split[:], 0.0).then_inc(split_done, 1)
            nc.vector.memset(ones[:], 1.0).then_inc(split_done, 1)
            nc.vector.memset(row_sum[:], 0.0).then_inc(sel_zeroed, 1)
            nc.vector.memset(prod[:, BODY - TILES:], 0.0).then_inc(consts_ready, 1)
            dve.wait_ge(sel_zeroed, 1)
            for k in range(BODY // TILES):
                for half in range(HALVES):
                    nc.vector.memset(row_sum[half * U:(half + 1) * U, k, 2 * k + half:2 * k + half + 1],
                                     1.0).then_inc(consts_ready, 1)
            dve.wait_ge(w_loaded, 16 * N_WEIGHT_DMAS)
            nc.vector.tensor_tensor(gate_bias[:, 0:2], biases[:, BI:BI + 2], biases[:, BR:BR + 2], ALU.add).then_inc(bias_ready, 1)
            dve.wait_ge(bias_ready, 1)
            nc.vector.tensor_scalar(gate_bias[:, 2:3], gate_bias[:, 0:1], -1.0, None, ALU.mult).then_inc(bias_ready, 1)
            nc.vector.tensor_copy(bias_part[:, 0], bias_rows[:]).then_inc(split_done, 1)
            dve.wait_ge(split_done, 3)
            nc.vector.tensor_tensor(bias_left[:, 0], bias_rows[:], bias_part[:, 0], ALU.subtract).then_inc(split_done, 1)
            dve.wait_ge(split_done, 4)
            nc.vector.tensor_copy(bias_part[:, 1], bias_left[:, 0]).then_inc(split_done, 1)
            dve.wait_ge(split_done, 5)
            nc.vector.tensor_tensor(bias_left[:, 1], bias_left[:, 0], bias_part[:, 1], ALU.subtract).then_inc(split_done, 1)
            dve.wait_ge(split_done, 6)
            nc.vector.tensor_copy(bias_part[:, 2], bias_left[:, 1]).then_inc(split_done, 1)
            dve.wait_ge(split_done, 7)
            for i in range(3):
                row = slice(QUAD * i, QUAD * i + 1)
                nc.vector.tensor_copy(bias_split[row], bias_part[row, i]).then_inc(split_done, 1)
            dve.wait_ge(qw_summed, 1)
            nc.vector.tensor_copy(qw[:], logit_bank[:, 0:COLS]).then_inc(qw_ready, 1)
            for g in GROUPS:
                for q in (gated_ready[g], cand_ready[g], new_ready[g], *agated_ready[g], *acand_ready[g], *anew_ready[g]):
                    dve.sem_inc(q, 1)
            for g in GROUPS:
                nc.vector.memset(h_at(-1)[:, gcols(g)], 0.0).then_inc(h_ready[g], 1)
                nc.vector.memset(state[:, 1, gcols(g)], 0.0).then_inc(s_ready[g], 1)

            def bank_parts(g):
                hid, inp = c_bank[g][:, 0:GC], c_bank[g][:, GC:2 * GC]
                cand, new = vec_bank[:, g * GC:(g + 1) * GC], vec_bank[:, (2 + g) * GC:(3 + g) * GC]
                return hid, inp, cand, new

            with dve.Fori(0, T, BODY) as t0:
                for s in range(BODY):
                    for g in GROUPS:
                        hid, inp, cand, new = bank_parts(g)
                        dve.wait_ge(rh_summed[g], t0 + (s + 2))
                        dve.wait_ge(r_ready[g], t0 + (s + 2))
                        nc.vector.scalar_tensor_tensor(gated[:, g], hid, biases[:, BR + 2:BR + 3], r_gate[:, g],
                                                       ALU.add, ALU.mult).then_inc(gated_ready[g], 1)
                        dve.wait_ge(gated_ready[g], t0 + (s + 2))
                        nc.vector.scalar_tensor_tensor(cand, inp, biases[:, BI + 2:BI + 3], gated[:, g],
                                                       ALU.add, ALU.add).then_inc(cand_ready[g], 1)
                        dve.wait_ge(cand_ready[g], t0 + (s + 2))
                        dve.wait_ge(zr_ready[g], t0 + (s + 2))
                        nc.vector.scalar_tensor_tensor(new, cand, 0.0, z_rest[:, g],
                                                       ALU.max, ALU.mult).then_inc(new_ready[g], 1)
                        if g == 0 and s % CHUNK == 0:
                            dve.wait_ge(outs_stored[s // CHUNK], t0 + 16)
                        dve.wait_ge(new_ready[g], t0 + (s + 2))
                        dve.wait_ge(kept_ready[g], t0 + (s + 2))
                        nc.vector.tensor_tensor(h_at(s)[:, gcols(g)], new, kept[:, g], ALU.add).then_inc(h_ready[g], 1)

            for n in range(N_COPY):
                dve.wait_ge(turned, n + 1)
                m, part = n // (TM // PER_COPY), n % (TM // PER_COPY)
                src = (r_bank + z_bank)[n % 4]
                nc.vector.tensor_copy(batch_rows[:, m, part * 512:(part + 1) * 512], src[:]).then_inc(turned_copied, 1)
            dve.wait_ge(turned_copied, N_COPY)
            for m in range(BM):
                nc.vector.reduce_max(softmax_stat[:, 0, m:m + 1], batch_rows[:, m], AX_X).then_inc(stat_ready, 1)
            dve.wait_ge(stat_ready, BM)
            nc.vector.tensor_scalar(softmax_stat[:, 1], softmax_stat[:, 0], -1.0, None, ALU.mult).then_inc(stat_ready, 1)
            dve.wait_ge(exp_ready, BM)
            nc.vector.reciprocal(softmax_stat[:, 3], softmax_stat[:, 2]).then_inc(stat_ready, 1)
            dve.wait_ge(stat_ready, BM + 2)
            for m in range(BM):
                nc.vector.tensor_scalar(batch_rows[:, m], batch_rows[:, m], softmax_stat[:, 3, m:m + 1], None,
                                        ALU.mult).then_inc(probs_ready, 1)
            for n in range(N_COPY):
                dve.wait_ge(back, n + 1)
                nc.vector.tensor_copy(time_rows[:, n, :], (r_bank + z_bank)[n % 4][:]).then_inc(back_copied, 1)

            with dve.Fori(0, T, BODY) as t0:
                for s in range(BODY):
                    for g in GROUPS:
                        hid, inp, cand, new = bank_parts(g)
                        dve.wait_ge(akept_ready[g], t0 + (s + 2))
                        dve.wait_ge(rc_summed[g], t0 + (s + 2))
                        dve.wait_ge(ar_ready[g], t0 + (s + 2))
                        for part, c in PARTS:
                            nc.vector.tensor_tensor(gated[:, g, c], hid[:, c], r_gate[:, g, c],
                                                    ALU.mult).then_inc(agated_ready[g][part], 1)
                        for part, c in PARTS:
                            dve.wait_ge(agated_ready[g][part], t0 + (s + 2))
                            nc.vector.tensor_tensor(cand[:, c], inp[:, c], gated[:, g, c],
                                                    ALU.add).then_inc(acand_ready[g][part], 1)
                        if g == 0 and s % CHUNK == 0:
                            dve.wait_ge(a_loaded[s // CHUNK], t0 * 2 + 32)
                        for part, c in PARTS:
                            dve.wait_ge(acand_ready[g][part], t0 + (s + 2))
                            nc.vector.scalar_tensor_tensor(new[:, c], cand[:, c], 0.0, attn_at(s)[:, gcols(g)][:, c],
                                                           ALU.max, ALU.mult).then_inc(anew_ready[g][part], 1)
                        for part, c in PARTS:
                            dve.wait_ge(anew_ready[g][part], t0 + (s + 2))
                            last = nc.vector.tensor_tensor(state[:, s % 2, gcols(g)][:, c], new[:, c],
                                                           kept[:, g, c], ALU.add)
                        last.then_inc(s_ready[g], 1)

        @block.tensor
        def _(pe):
            pe.wait_ge(w_loaded, 16 * N_WEIGHT_DMAS)
            nc.tensor.matmul(logit_bank[:, 0:COLS], weights[:, ATT], q_t[:], start=True, stop=True).then_inc(qw_summed, 1)
            for g in GROUPS:
                for q in (r_summed[g], rh_summed[g], z_summed[g], ar_summed[g], rc_summed[g]):
                    pe.sem_inc(q, 1)
            pe.wait_ge(qw_ready, 1)
            pe.sem_inc(logits_summed, BODY)
            pe.wait_ge(consts_ready, 2 * BODY // TILES + 1)

            def mm(dst, w, moving, start, stop):
                return nc.tensor.matmul(dst, weights[:, w], moving, start=start, stop=stop, skip_group_check=True)

            def logit(s, last):
                j, k = s % TILES, s // TILES
                return nc.tensor.matmul(logit_bank[32 * j:32 * (j + 1), 0:COLS], row_sum[:, k], prod[:, s],
                                        start=(k == 0), stop=last, skip_group_check=True)

            def sum_logits(first):
                for s in range(first, first + TILES):
                    last = logit(s, s >= BODY - TILES)
                last.then_inc(logits_summed, TILES)

            with pe.Fori(0, T, BODY) as t0:
                for s in range(BODY):
                    if s % TILES == 1:
                        for g in GROUPS:
                            pe.wait_ge(prod_ready[g], t0 + s)
                        if s == 1 + TILES:
                            pe.wait_ge(logits_copied, t0 + BODY)
                        sum_logits((s - 1 - TILES) % BODY)
                    for g in GROUPS:
                        xs, hs = x_at(s)[:, gcols(g)], h_at(s - 1)[:, gcols(g)]
                        if g == 0 and s % CHUNK == 0:
                            pe.wait_ge(x_loaded[s // CHUNK], t0 + 16)
                        pe.wait_ge(r_ready[g], t0 + (s + 1))
                        mm(r_bank[g][:, 0:GC], GX_R, xs, True, False)
                        pe.wait_ge(zr_ready[g], t0 + (s + 1))
                        mm(z_bank[g][:, 0:GC], GX_Z, xs, True, False)
                        pe.wait_ge(cand_ready[g], t0 + (s + 1))
                        last = mm(c_bank[g][:, GC:2 * GC], GX_H, xs, True, False)
                        if g == 1 and s % CHUNK == CHUNK - 1:
                            last.then_inc(x_used, CHUNK)
                        pe.wait_ge(h_ready[g], t0 + (s + 1))
                        mm(r_bank[g][:, 0:GC], GH_R, hs, False, True).then_inc(r_summed[g], 1)
                        mm(c_bank[g][:, 0:GC], GH_H, hs, False, True).then_inc(rh_summed[g], 1)
                        mm(z_bank[g][:, 0:GC], GH_Z, hs, False, True).then_inc(z_summed[g], 1)
            for g in GROUPS:
                pe.wait_ge(prod_ready[g], T + 1)
            sum_logits(BODY - TILES)
            for g in GROUPS:
                pe.wait_ge(prod_ready[g], T + 2)
            pe.wait_ge(logits_copied, T + BODY)
            logit(0, True).then_inc(logits_summed, 1)

            pe.wait_ge(id_ready, 1)
            pe.wait_ge(rows_loaded, 16 * HALVES)
            for n in range(N_COPY):
                if n == 0:
                    for g in GROUPS:
                        pe.wait_ge(zr_ready[g], T + 1)
                if n >= 4:
                    pe.wait_ge(turned_copied, n - 3)
                dst = (r_bank + z_bank)[n % 4]
                for k in range(PER_COPY):
                    m, tm = n // (TM // PER_COPY), n % (TM // PER_COPY) * PER_COPY + k
                    last = nc.tensor.transpose(dst[:, k * P:(k + 1) * P], time_rows[:, tm, m * P:(m + 1) * P], ident[:])
                last.then_inc(turned, 1)
            for n in range(N_COPY):
                if n == 0:
                    pe.wait_ge(probs_ready, BM)
                if n >= 4:
                    pe.wait_ge(back_copied, n - 3)
                dst = (r_bank + z_bank)[n % 4]
                for m in range(BM):
                    last = nc.tensor.transpose(dst[:, m * P:(m + 1) * P], batch_rows[:, m, n * P:(n + 1) * P], ident[:])
                last.then_inc(back, 1)
            pe.wait_ge(back_copied, N_COPY)

            pe.wait_ge(split_done, 10)

            def add_bias(dst, part):
                return nc.tensor.matmul(dst, bias_split[:, part], ones[:], start=False, stop=False,
                                        skip_group_check=True)

            with pe.Fori(0, T, BODY) as t0:
                for s in range(BODY):
                    for g in GROUPS:
                        xs, hs = x_at(s)[:, gcols(g)], state[:, (s - 1) % 2, gcols(g)]
                        if g == 0 and s % CHUNK == 0:
                            pe.wait_ge(x_loaded[s // CHUNK], t0 + (T + 16))
                        pe.wait_ge(ar_ready[g], t0 + (s + 1))
                        mm(r_bank[g][:, 0:GC], AX_R, xs, True, False)
                        add_bias(r_bank[g][:, 0:GC], 0)
                        pe.wait_ge(acand_ready[g][1], t0 + (s + 1))
                        last = mm(c_bank[g][:, GC:2 * GC], AX_C, xs, True, False)
                        if g == 1 and s % CHUNK == CHUNK - 1:
                            last.then_inc(x_used, CHUNK)
                        add_bias(c_bank[g][:, GC:2 * GC], 1)
                        pe.wait_ge(s_ready[g], t0 + (s + 1))
                        mm(r_bank[g][:, 0:GC], AH_R, hs, False, True).then_inc(ar_summed[g], 1)
                        mm(c_bank[g][:, 0:GC], AH_C, hs, False, True).then_inc(rc_summed[g], 1)


def kernel(r_keys, r_queries, L0_rec_W_att, L0_rec_gru_Wx, L0_rec_gru_Wh, L0_rec_gru_b_in, L0_rec_gru_b_rec,
           L0_rec_agru_Wx, L0_rec_agru_Wh, L0_rec_agru_b):
    import numpy as np
    import concourse.bacc as bacc
    from concourse.bass_utils import run_bass_kernel_spmd

    B, T, E = r_keys.shape
    half = B // 2
    keys = np.asarray(r_keys).reshape(2, half, T // CHUNK, CHUNK, E)
    arrays = {
        "keys_t": keys.transpose(2, 0, 4, 3, 1).reshape(T // CHUNK, 2 * E, CHUNK * half),
        "queries_t": np.asarray(r_queries).reshape(2, half, -1).transpose(0, 2, 1).reshape(-1, half),
        "w_att_t": np.asarray(L0_rec_W_att).T,
        "gru_wx": np.asarray(L0_rec_gru_Wx),
        "gru_wh": np.asarray(L0_rec_gru_Wh),
        "gru_b_in": np.asarray(L0_rec_gru_b_in).reshape(3, -1).T,
        "gru_b_rec": np.asarray(L0_rec_gru_b_rec).reshape(3, -1).T,
        "agru_wx": np.asarray(L0_rec_agru_Wx),
        "agru_wh": np.asarray(L0_rec_agru_Wh),
        "agru_b": np.asarray(L0_rec_agru_b).reshape(2, -1).T,
        "agru_b_row": np.tile(np.asarray(L0_rec_agru_b).reshape(1, 2, 1, E), (1, 1, 2, 1)).reshape(1, 2, 2 * E),
    }
    arrays = {k: np.ascontiguousarray(v) for k, v in arrays.items()}
    nc = bacc.Bacc("TRN2", target_bir_lowering=False, num_devices=1)
    args = [nc.dram_tensor(f"in_{k}", v.shape, F32, kind="ExternalInput").ap() for k, v in arrays.items()]
    out = nc.dram_tensor("out_state", (2 * E, half), F32, kind="ExternalOutput").ap()
    recurrent_attention_kernel(nc, *args, out)
    r = run_bass_kernel_spmd(nc, [{f"in_{k}": v for k, v in arrays.items()}], core_ids=[0])
    state = r.results[0]["out_state"]
    return np.ascontiguousarray(state.reshape(2, E, half).transpose(0, 2, 1).reshape(B, E))
```

```python
from contextlib import ExitStack

import concourse.bass as bass
from concourse import mybir

F32 = mybir.dt.float32
BF16 = mybir.dt.bfloat16
QUAD = 32
ALU = mybir.AluOpType
ACT = mybir.ActivationFunctionType
AX_X = mybir.AxisListType.X

P = 128
CHUNK = 8
BODY = 2 * CHUNK
DMA = 16
TILES = 4


def recurrent_attention_kernel(nc, keys_t, queries_t, weight_columns, bias_columns, agru_b_row, out):
    n_chunks, _, chunk_cols = keys_t.shape
    U = weight_columns.shape[0]
    COLS = chunk_cols // CHUNK
    T = n_chunks * CHUNK
    GC = COLS // 2
    GROUPS = (0, 1)
    HALVES = P // U
    TM = T // P
    BM = HALVES * COLS // P
    assert HALVES == 2 and GC == P and T % BODY == 0 and BODY == DMA

    BODIES = T // BODY
    ROW0 = BODY + 1
    outs_dram = nc.dram_tensor("gru_outputs", (BODIES, 2, P, CHUNK, COLS), F32).ap()
    logits_dram = nc.dram_tensor("logits", (T + ROW0, HALVES, COLS), F32).ap()
    attn_dram = nc.dram_tensor("attention", (HALVES, T, COLS), F32).ap()
    keys = keys_t.rearrange("(k b) p (s c) -> k b p s c", b=2, s=CHUNK)
    attn_bodies = attn_dram.rearrange("h (k b s) c -> k b h s c", b=2, s=CHUNK)
    logit_bodies = logits_dram[0:T + BODY].rearrange("(k i j) h c -> k j i h c", j=TILES, i=BODY // TILES)

    with ExitStack() as ctx:
        def sb(name, shape):
            return ctx.enter_context(nc.sbuf_tensor(name, shape, F32))

        def bank(name):
            return ctx.enter_context(nc.psum_tensor(name, [P, 512], F32))

        def sem(name):
            return ctx.enter_context(nc.semaphore(name))

        def sems(name):
            return [sem(f"{name}_{'ab'[g]}") for g in GROUPS]

        weights = sb("weights", [P, 11, P])
        GX_Z, GX_R, GX_H, GH_Z, GH_R, GH_H, AX_R, AX_C, AH_R, AH_C, ATT = range(11)
        biases = sb("biases", [P, 8])
        BI, BR, BA = 0, 3, 6
        gate_bias = sb("gate_bias", [P, 3])
        q_t = sb("q_t", [P, COLS])
        qw = sb("qw", [P, COLS])
        ident = sb("ident", [P, P])
        bias_rows = sb("bias_rows", [P, 2, P])
        bias_part = ctx.enter_context(nc.sbuf_tensor("bias_part", [P, 3, 2, P], BF16))
        bias_left = sb("bias_left", [P, 2, 2, P])
        bias_split = ctx.enter_context(nc.sbuf_tensor("bias_split", [P, 2, P], BF16))
        ones = ctx.enter_context(nc.sbuf_tensor("ones", [P, GC], BF16))
        row_sum = sb("row_sum", [P, BODY // TILES, 32])
        x = sb("x", [P, 2, CHUNK, COLS])
        h = sb("h", [P, 2, CHUNK, COLS])
        r_gate = sb("r_gate", [P, 2, GC])
        z_gate = sb("z_gate", [P, 2, GC])
        z_rest = sb("z_rest", [P, 2, GC])
        gated = sb("gated", [P, 2, GC])
        kept = sb("kept", [P, 2, GC])
        prod = sb("prod", [P, BODY, COLS])
        logit_rows = sb("logit_rows", [P, COLS])
        time_rows = sb("time_rows", [P, TM, HALVES * COLS])
        batch_rows = sb("batch_rows", [P, BM, T])
        softmax_stat = sb("softmax_stat", [P, 4, BM])
        attn = sb("attn", [P, 2, CHUNK, COLS])
        attn_rest = sb("attn_rest", [P, 2, COLS])
        state = sb("state", [P, 2, COLS])

        r_bank = [bank(f"r_bank_{'ab'[g]}") for g in GROUPS]
        z_bank = [bank(f"z_bank_{'ab'[g]}") for g in GROUPS]
        c_bank = [bank(f"c_bank_{'ab'[g]}") for g in GROUPS]
        logit_bank = bank("logit_bank")
        vec_bank = bank("vec_bank")

        w_zeroed, w_loaded, consts_ready = sem("w_zeroed"), sem("w_loaded"), sem("consts_ready")
        qw_summed, qw_ready, bias_ready = sem("qw_summed"), sem("qw_ready"), sem("bias_ready")
        id_zeroed, id_ready, sel_zeroed = sem("id_zeroed"), sem("id_ready"), sem("sel_zeroed")
        x_loaded = [sem("x_loaded_0"), sem("x_loaded_1")]
        x_used = sem("x_used")
        h_ready, r_summed, rh_summed, z_summed = sems("h_ready"), sems("r_summed"), sems("rh_summed"), sems("z_summed")
        r_ready, z_ready, zr_ready = sems("r_ready"), sems("z_ready"), sems("z_rest_ready")
        gated_ready, cand_ready, new_ready = sems("gated_ready"), sems("cand_ready"), sems("new_ready")
        kept_ready, prod_ready = sems("kept_ready"), sems("prod_ready")
        outs_stored = [sem("outs_stored_0"), sem("outs_stored_1")]
        logits_summed, logits_copied, logits_stored = sem("logits_summed"), sem("logits_copied"), sem("logits_stored")
        rows_loaded = [sem("rows_loaded_early"), sem("rows_loaded_last")]
        turned, turned_copied, max_ready = sem("turned"), sem("turned_copied"), sem("max_ready")
        stat_ready, exp_ready, probs_ready = sem("stat_ready"), sem("exp_ready"), sem("probs_ready")
        back, back_copied, back_copied_late = sem("back"), sem("back_copied"), sem("back_copied_late")
        attn_stored = [sem("attn_stored_first"), sem("attn_stored_rest")]
        a_loaded = [sem("a_loaded_0"), sem("a_loaded_1")]
        s_ready, ar_summed, rc_summed = sems("s_ready"), sems("ar_summed"), sems("rc_summed")
        ar_ready, rest_ready = sems("ar_ready"), sem("rest_ready")
        akept_ready = sems("akept_ready")
        agated_ready, acand_ready, anew_ready = (
            [[sem(f"{name}_{'ab'[g]}{part}") for part in range(2)] for g in GROUPS]
            for name in ("agated_ready", "acand_ready", "anew_ready"))
        split_done = sem("split_done")
        out_stored, table_loaded = sem("out_stored"), sem("table_loaded")

        PARTS = ((0, slice(0, GC // 2)), (1, slice(GC // 2, GC)))

        def gcols(g):
            return slice(g * GC, (g + 1) * GC)

        def h_at(s):
            s = s % BODY
            return h[:, s // CHUNK, s % CHUNK, :]

        def x_at(s):
            return x[:, s // CHUNK, s % CHUNK, :]

        def attn_at(s):
            return attn[:, s // CHUNK, s % CHUNK, :]

        N_WEIGHT_DMAS = 2 * HALVES + 1 + 3
        N_TURN = TM * BM
        PER_COPY = 4
        N_COPY = N_TURN // PER_COPY
        assert TM == 2 * PER_COPY and BM == 4

        def turn_bank(n):
            return (r_bank + z_bank)[n % 4]

        block = ctx.enter_context(nc.Block())

        @block.sync
        def _(sp):
            def chunk_of(dram, k, b):
                return dram[k, b] if isinstance(k, int) else dram[bass.ds(k, 1), b].rearrange("a p s c -> (a p) s c")

            def load_x(dram, k, b):
                sp.dma_start(x[:, b], chunk_of(dram, k, b)).then_inc(x_loaded[b], DMA)

            def store_outs(k, b):
                for g in GROUPS:
                    sp.wait_ge(h_ready[g], k * BODY + (CHUNK * (b + 1) + 1))
                sp.dma_start(chunk_of(outs_dram, k, b), h[:, b]).then_inc(outs_stored[b], DMA)

            def store_logits(k):
                sp.wait_ge(logits_copied, k * BODY + BODY)
                for j in range(TILES):
                    dst = (logit_bodies[k, j] if isinstance(k, int)
                           else logit_bodies[bass.ds(k, 1), j].rearrange("a i h c -> (a i) h c"))
                    sp.dma_start(dst, logit_rows[32 * j:32 * j + 2 * BODY // TILES, :]).then_inc(logits_stored, DMA)

            def load_attn(k, b):
                for half in range(HALVES):
                    src = (attn_bodies[k, b, half].rearrange("(a s) c -> a s c", a=1) if isinstance(k, int)
                           else attn_bodies[bass.ds(k, 1), b, half])
                    sp.dma_start(attn[half * U:(half + 1) * U, b],
                                 src.broadcast_to((U, CHUNK, COLS))).then_inc(a_loaded[b], DMA)

            for b in range(2):
                load_x(keys, 0, b)
            for half in range(HALVES):
                rows = slice(half * U, (half + 1) * U)
                sp.dma_start(biases[rows], bias_columns).then_inc(w_loaded, DMA)
            sp.dma_start(q_t[:], queries_t).then_inc(w_loaded, DMA)
            sp.wait_ge(w_zeroed, 2)
            for half in range(HALVES):
                rows = slice(half * U, (half + 1) * U)
                sp.dma_start(weights[rows, :, rows], weight_columns.rearrange("k (n u) -> k n u", u=U)).then_inc(w_loaded, DMA)
            for i in range(3):
                sp.dma_start(bias_rows[QUAD * i:QUAD * i + 1], agru_b_row).then_inc(w_loaded, DMA)
            for b in range(2):
                sp.sem_inc(outs_stored[b], DMA)
            sp.sem_inc(logits_stored, DMA * TILES)
            with sp.Fori(0, BODIES - 1) as k:
                for b in range(2):
                    sp.wait_ge(x_used, k * BODY + CHUNK * (b + 1))
                    load_x(keys, k + 1, b)
                    store_outs(k, b)
                store_logits(k)
            def load_rows(m0, m1, part):
                for half in range(HALVES):
                    sp.dma_start(time_rows[:, m0:m1, half * COLS:(half + 1) * COLS],
                                 logits_dram[ROW0 + m0 * P:ROW0 + m1 * P, half].rearrange("(m p) c -> p m c", p=P)
                                 ).then_inc(rows_loaded[part], DMA)

            EARLY_BODIES = -(-(ROW0 + (TM - 1) * P) // BODY)
            sp.wait_ge(logits_stored, DMA * TILES * (EARLY_BODIES + 1))
            load_rows(0, TM - 1, 0)
            for b in range(2):
                store_outs(BODIES - 1, b)
            store_logits(BODIES - 1)
            store_logits(BODIES)
            sp.wait_ge(logits_copied, T + BODY + 1)
            sp.dma_start(logits_dram[T + BODY], logit_rows[0:HALVES, :]).then_inc(logits_stored, DMA)

            sp.wait_ge(logits_stored, DMA * (TILES * (BODIES + 2) + 1))
            load_rows(TM - 1, TM, 1)
            for b in range(2):
                sp.wait_ge(outs_stored[b], DMA * (BODIES + 1))
            sp.wait_ge(x_used, T)
            for b in range(2):
                load_x(outs_dram, 0, b)
            for half in range(HALVES):
                sp.wait_ge(back_copied, (half + 1) * BM // HALVES)
                sp.wait_ge(back_copied_late, (half + 1) * BM // HALVES)
                for m0, m1, part in ((0, 1, 0), (1, TM, 1)):
                    sp.dma_start(attn_dram[half, m0 * P:m1 * P].rearrange("(m p) c -> p m c", p=P),
                                 time_rows[:, m0:m1, half * COLS:(half + 1) * COLS]).then_inc(attn_stored[part], DMA)
            sp.wait_ge(attn_stored[0], DMA * HALVES)
            for b in range(2):
                load_attn(0, b)
            sp.wait_ge(attn_stored[1], DMA * HALVES)
            with sp.Fori(0, BODIES - 1) as k:
                for b in range(2):
                    sp.wait_ge(x_used, k * BODY + (T + CHUNK * (b + 1)))
                    load_x(outs_dram, k + 1, b)
                    for g in GROUPS:
                        sp.wait_ge(anew_ready[g][1], k * BODY + (CHUNK * (b + 1) + 1))
                    sp.wait_ge(rest_ready, k * BODY + (CHUNK * (b + 1) + 1))
                    load_attn(k + 1, b)
            for g in GROUPS:
                sp.wait_ge(s_ready[g], T + 1)
            sp.dma_start(out, state[:, (T - 1) % 2, :]).then_inc(out_stored, DMA)
            sp.wait_ge(out_stored, DMA)

        @block.gpsimd
        def _(pool):
            nc.gpsimd.memset(ident[:], 0.0).then_inc(id_zeroed, 1)
            pool.wait_ge(id_zeroed, 1)
            nc.gpsimd.affine_select(out=ident[:], in_=ident[:], compare_op=ALU.not_equal, fill=1.0, base=0,
                                    pattern=[[-1, P]], channel_multiplier=1).then_inc(id_ready, 1)
            for g in GROUPS:
                pool.sem_inc(kept_ready[g], 1)
                pool.sem_inc(prod_ready[g], 1)
                pool.sem_inc(akept_ready[g], 1)
            pool.wait_ge(qw_ready, 1)

            def product(s, g):
                nc.gpsimd.tensor_tensor(prod[:, s, gcols(g)], h_at(s - 1)[:, gcols(g)], qw[:, gcols(g)],
                                        ALU.mult).then_inc(prod_ready[g], 1)

            with pool.Fori(0, T, BODY) as t0:
                for s in range(BODY):
                    for g in GROUPS:
                        pool.wait_ge(z_ready[g], t0 + (s + 2))
                        nc.gpsimd.tensor_tensor(kept[:, g], z_gate[:, g], h_at(s - 1)[:, gcols(g)],
                                                ALU.mult).then_inc(kept_ready[g], 1)
                        if g == 0 and s % TILES == 0:
                            pool.wait_ge(logits_summed, t0 + (s + 2 * TILES))
                        product(s, g)
            pool.wait_ge(logits_summed, T + 2 * TILES)
            for g in GROUPS:
                pool.wait_ge(h_ready[g], T + 1)
                product(0, g)

            with pool.Fori(0, T, BODY) as t0:
                for s in range(BODY):
                    for g in GROUPS:
                        if g == 0:
                            pool.wait_ge(rest_ready, t0 + (s + 2))
                        pool.wait_ge(s_ready[g], t0 + (s + 1))
                        nc.gpsimd.tensor_tensor(kept[:, g], attn_rest[:, s % 2, gcols(g)],
                                                state[:, (s - 1) % 2, gcols(g)], ALU.mult).then_inc(akept_ready[g], 1)

        @block.scalar
        def _(act):
            for g in GROUPS:
                for q in (r_ready[g], z_ready[g], zr_ready[g], ar_ready[g]):
                    act.sem_inc(q, 1)
            act.sem_inc(rest_ready, 1)
            act.wait_ge(bias_ready, 2)
            nc.scalar.activation(r_gate[:, 0, 0:1], gate_bias[:, 0:1], ACT.Sigmoid).then_inc(table_loaded, 1)
            act.wait_ge(table_loaded, 1)

            def copy_logits(t0):
                act.wait_ge(logits_summed, t0 + (BODY + TILES))
                act.wait_ge(logits_stored, t0 * (DMA * TILES // BODY) + DMA * TILES)
                nc.scalar.activation(logit_rows[:], logit_bank[:, 0:COLS], ACT.Copy).then_inc(logits_copied, BODY)

            with act.Fori(0, T, BODY) as t0:
                for s in range(BODY):
                    for g in GROUPS:
                        act.wait_ge(r_summed[g], t0 + (s + 2))
                        nc.scalar.activation(r_gate[:, g], r_bank[g][:, 0:GC], ACT.Sigmoid,
                                             bias=gate_bias[:, 1:2]).then_inc(r_ready[g], 1)
                        act.wait_ge(z_summed[g], t0 + (s + 2))
                        nc.scalar.activation(z_gate[:, g], z_bank[g][:, 0:GC], ACT.Sigmoid,
                                             bias=gate_bias[:, 0:1]).then_inc(z_ready[g], 1)
                        nc.scalar.activation(z_rest[:, g], z_bank[g][:, 0:GC], ACT.Sigmoid, scale=-1.0,
                                             bias=gate_bias[:, 2:3]).then_inc(zr_ready[g], 1)
                    if s == 2:
                        copy_logits(t0)
            copy_logits(T)
            act.wait_ge(logits_summed, T + BODY + TILES + 1)
            act.wait_ge(logits_stored, DMA * TILES * (BODIES + 2))
            nc.scalar.activation(logit_rows[0:32], logit_bank[0:32, 0:COLS], ACT.Copy).then_inc(logits_copied, 1)

            for m in range(BM):
                act.wait_ge(stat_ready, m + 1)
                nc.scalar.activation(batch_rows[:, m], batch_rows[:, m], ACT.Exp, bias=softmax_stat[:, 1, m:m + 1],
                                     accum_out=softmax_stat[:, 2, m:m + 1]).then_inc(exp_ready, 1)
            nc.scalar.activation(r_gate[:, 0, 0:1], gate_bias[:, 0:1], ACT.Sigmoid).then_inc(table_loaded, 1)
            act.wait_ge(table_loaded, 2)
            for m in range(BM):
                act.wait_ge(back, 2 * m + 2)
                nc.scalar.activation(time_rows[:, PER_COPY:, m * P:(m + 1) * P],
                                     turn_bank(2 * m + 1)[:].rearrange("p (k c) -> p k c", k=PER_COPY),
                                     ACT.Copy).then_inc(back_copied_late, 1)

            with act.Fori(0, T, BODY) as t0:
                for s in range(BODY):
                    if s % CHUNK == 0:
                        act.wait_ge(a_loaded[s // CHUNK], t0 * (DMA * HALVES // BODY) + DMA * HALVES)
                    nc.scalar.activation(attn_rest[:, s % 2], attn_at(s), ACT.Copy, bias=1.0,
                                         scale=-1.0).then_inc(rest_ready, 1)
                    for g in GROUPS:
                        act.wait_ge(ar_summed[g], t0 + (s + 2))
                        nc.scalar.activation(r_gate[:, g], r_bank[g][:, 0:GC], ACT.Sigmoid).then_inc(ar_ready[g], 1)

        @block.vector
        def _(dve):
            nc.vector.memset(weights[:], 0.0).then_inc(w_zeroed, 1)
            nc.vector.memset(bias_rows[:], 0.0).then_inc(w_zeroed, 1)
            nc.vector.memset(bias_split[:], 0.0).then_inc(split_done, 1)
            nc.vector.memset(ones[:], 1.0).then_inc(split_done, 1)
            nc.vector.memset(row_sum[:], 0.0).then_inc(sel_zeroed, 1)
            nc.vector.memset(prod[:, BODY - TILES:], 0.0).then_inc(consts_ready, 1)
            dve.wait_ge(sel_zeroed, 1)
            for k in range(BODY // TILES):
                for half in range(HALVES):
                    nc.vector.memset(row_sum[half * U:(half + 1) * U, k, 2 * k + half:2 * k + half + 1],
                                     1.0).then_inc(consts_ready, 1)
            dve.wait_ge(w_loaded, DMA * N_WEIGHT_DMAS)
            nc.vector.tensor_tensor(gate_bias[:, 0:2], biases[:, BI:BI + 2], biases[:, BR:BR + 2], ALU.add).then_inc(bias_ready, 1)
            dve.wait_ge(bias_ready, 1)
            nc.vector.tensor_scalar(gate_bias[:, 2:3], gate_bias[:, 0:1], -1.0, None, ALU.mult).then_inc(bias_ready, 1)
            nc.vector.tensor_copy(bias_part[:, 0], bias_rows[:]).then_inc(split_done, 1)
            dve.wait_ge(split_done, 3)
            nc.vector.tensor_tensor(bias_left[:, 0], bias_rows[:], bias_part[:, 0], ALU.subtract).then_inc(split_done, 1)
            dve.wait_ge(split_done, 4)
            nc.vector.tensor_copy(bias_part[:, 1], bias_left[:, 0]).then_inc(split_done, 1)
            dve.wait_ge(split_done, 5)
            nc.vector.tensor_tensor(bias_left[:, 1], bias_left[:, 0], bias_part[:, 1], ALU.subtract).then_inc(split_done, 1)
            dve.wait_ge(split_done, 6)
            nc.vector.tensor_copy(bias_part[:, 2], bias_left[:, 1]).then_inc(split_done, 1)
            dve.wait_ge(split_done, 7)
            for i in range(3):
                row = slice(QUAD * i, QUAD * i + 1)
                nc.vector.tensor_copy(bias_split[row], bias_part[row, i]).then_inc(split_done, 1)
            dve.wait_ge(qw_summed, 1)
            nc.vector.tensor_copy(qw[:], logit_bank[:, 0:COLS]).then_inc(qw_ready, 1)
            for g in GROUPS:
                for q in (gated_ready[g], cand_ready[g], new_ready[g], *agated_ready[g], *acand_ready[g], *anew_ready[g]):
                    dve.sem_inc(q, 1)
            for g in GROUPS:
                nc.vector.memset(h_at(-1)[:, gcols(g)], 0.0).then_inc(h_ready[g], 1)
                nc.vector.memset(state[:, 1, gcols(g)], 0.0).then_inc(s_ready[g], 1)

            def bank_parts(g):
                hid, inp = c_bank[g][:, 0:GC], c_bank[g][:, GC:2 * GC]
                cand, new = vec_bank[:, g * GC:(g + 1) * GC], vec_bank[:, (2 + g) * GC:(3 + g) * GC]
                return hid, inp, cand, new

            with dve.Fori(0, T, BODY) as t0:
                for s in range(BODY):
                    for g in GROUPS:
                        hid, inp, cand, new = bank_parts(g)
                        dve.wait_ge(rh_summed[g], t0 + (s + 2))
                        dve.wait_ge(r_ready[g], t0 + (s + 2))
                        nc.vector.scalar_tensor_tensor(gated[:, g], hid, biases[:, BR + 2:BR + 3], r_gate[:, g],
                                                       ALU.add, ALU.mult).then_inc(gated_ready[g], 1)
                        dve.wait_ge(gated_ready[g], t0 + (s + 2))
                        nc.vector.scalar_tensor_tensor(cand, inp, biases[:, BI + 2:BI + 3], gated[:, g],
                                                       ALU.add, ALU.add).then_inc(cand_ready[g], 1)
                        dve.wait_ge(cand_ready[g], t0 + (s + 2))
                        dve.wait_ge(zr_ready[g], t0 + (s + 2))
                        nc.vector.scalar_tensor_tensor(new, cand, 0.0, z_rest[:, g],
                                                       ALU.max, ALU.mult).then_inc(new_ready[g], 1)
                        if g == 0 and s % CHUNK == 0:
                            dve.wait_ge(outs_stored[s // CHUNK], t0 + DMA)
                        dve.wait_ge(new_ready[g], t0 + (s + 2))
                        dve.wait_ge(kept_ready[g], t0 + (s + 2))
                        nc.vector.tensor_tensor(h_at(s)[:, gcols(g)], new, kept[:, g], ALU.add).then_inc(h_ready[g], 1)

            for n in range(N_COPY):
                part, m = n // BM, n % BM
                dve.wait_ge(turned, n + 1)
                nc.vector.tensor_copy(batch_rows[:, m, part * 512:(part + 1) * 512],
                                      turn_bank(n)[:]).then_inc(turned_copied, 1)
                if part == 1:
                    dve.wait_ge(turned_copied, n + 1)
                    nc.vector.reduce_max(softmax_stat[:, 0, m:m + 1], batch_rows[:, m], AX_X).then_inc(max_ready, 1)
                    dve.wait_ge(max_ready, m + 1)
                    nc.vector.tensor_scalar(softmax_stat[:, 1, m:m + 1], softmax_stat[:, 0, m:m + 1], -1.0, None,
                                            ALU.mult).then_inc(stat_ready, 1)
            for m in range(BM):
                dve.wait_ge(exp_ready, m + 1)
                nc.vector.reciprocal(softmax_stat[:, 3, m:m + 1], softmax_stat[:, 2, m:m + 1]).then_inc(stat_ready, 1)
                dve.wait_ge(stat_ready, BM + m + 1)
                nc.vector.tensor_scalar(batch_rows[:, m], batch_rows[:, m], softmax_stat[:, 3, m:m + 1], None,
                                        ALU.mult).then_inc(probs_ready, 1)
            for m in range(BM):
                dve.wait_ge(back, 2 * m + 1)
                nc.vector.tensor_copy(time_rows[:, 0:PER_COPY, m * P:(m + 1) * P],
                                      turn_bank(2 * m)[:].rearrange("p (k c) -> p k c", k=PER_COPY)
                                      ).then_inc(back_copied, 1)

            with dve.Fori(0, T, BODY) as t0:
                for s in range(BODY):
                    for g in GROUPS:
                        hid, inp, cand, new = bank_parts(g)
                        dve.wait_ge(akept_ready[g], t0 + (s + 2))
                        dve.wait_ge(rc_summed[g], t0 + (s + 2))
                        dve.wait_ge(ar_ready[g], t0 + (s + 2))
                        for part, c in PARTS:
                            nc.vector.tensor_tensor(gated[:, g, c], hid[:, c], r_gate[:, g, c],
                                                    ALU.mult).then_inc(agated_ready[g][part], 1)
                        for part, c in PARTS:
                            dve.wait_ge(agated_ready[g][part], t0 + (s + 2))
                            nc.vector.tensor_tensor(cand[:, c], inp[:, c], gated[:, g, c],
                                                    ALU.add).then_inc(acand_ready[g][part], 1)
                        if g == 0 and s % CHUNK == 0:
                            dve.wait_ge(a_loaded[s // CHUNK], t0 * (DMA * HALVES // BODY) + DMA * HALVES)
                        for part, c in PARTS:
                            dve.wait_ge(acand_ready[g][part], t0 + (s + 2))
                            nc.vector.scalar_tensor_tensor(new[:, c], cand[:, c], 0.0, attn_at(s)[:, gcols(g)][:, c],
                                                           ALU.max, ALU.mult).then_inc(anew_ready[g][part], 1)
                        for part, c in PARTS:
                            dve.wait_ge(anew_ready[g][part], t0 + (s + 2))
                            last = nc.vector.tensor_tensor(state[:, s % 2, gcols(g)][:, c], new[:, c],
                                                           kept[:, g, c], ALU.add)
                        last.then_inc(s_ready[g], 1)

        @block.tensor
        def _(pe):
            pe.wait_ge(w_loaded, DMA * N_WEIGHT_DMAS)
            nc.tensor.matmul(logit_bank[:, 0:COLS], weights[:, ATT], q_t[:], start=True, stop=True).then_inc(qw_summed, 1)
            for g in GROUPS:
                for q in (r_summed[g], rh_summed[g], z_summed[g], ar_summed[g], rc_summed[g]):
                    pe.sem_inc(q, 1)
            pe.wait_ge(qw_ready, 1)
            pe.sem_inc(logits_summed, BODY)
            pe.wait_ge(consts_ready, 2 * BODY // TILES + 1)

            def mm(dst, w, moving, start, stop):
                return nc.tensor.matmul(dst, weights[:, w], moving, start=start, stop=stop, skip_group_check=True)

            def logit(s, last):
                j, k = s % TILES, s // TILES
                return nc.tensor.matmul(logit_bank[32 * j:32 * (j + 1), 0:COLS], row_sum[:, k], prod[:, s],
                                        start=(k == 0), stop=last, skip_group_check=True)

            def sum_logits(first):
                for s in range(first, first + TILES):
                    last = logit(s, s >= BODY - TILES)
                last.then_inc(logits_summed, TILES)

            with pe.Fori(0, T, BODY) as t0:
                for s in range(BODY):
                    if s % TILES == 1:
                        for g in GROUPS:
                            pe.wait_ge(prod_ready[g], t0 + s)
                        if s == 1 + TILES:
                            pe.wait_ge(logits_copied, t0 + BODY)
                        sum_logits((s - 1 - TILES) % BODY)
                    for g in GROUPS:
                        xs, hs = x_at(s)[:, gcols(g)], h_at(s - 1)[:, gcols(g)]
                        if g == 0 and s % CHUNK == 0:
                            pe.wait_ge(x_loaded[s // CHUNK], t0 + DMA)
                        pe.wait_ge(r_ready[g], t0 + (s + 1))
                        mm(r_bank[g][:, 0:GC], GX_R, xs, True, False)
                        pe.wait_ge(zr_ready[g], t0 + (s + 1))
                        mm(z_bank[g][:, 0:GC], GX_Z, xs, True, False)
                        pe.wait_ge(cand_ready[g], t0 + (s + 1))
                        last = mm(c_bank[g][:, GC:2 * GC], GX_H, xs, True, False)
                        if g == 1 and s % CHUNK == CHUNK - 1:
                            last.then_inc(x_used, CHUNK)
                        pe.wait_ge(h_ready[g], t0 + (s + 1))
                        mm(r_bank[g][:, 0:GC], GH_R, hs, False, True).then_inc(r_summed[g], 1)
                        mm(c_bank[g][:, 0:GC], GH_H, hs, False, True).then_inc(rh_summed[g], 1)
                        mm(z_bank[g][:, 0:GC], GH_Z, hs, False, True).then_inc(z_summed[g], 1)
            for g in GROUPS:
                pe.wait_ge(prod_ready[g], T + 1)
            sum_logits(BODY - TILES)
            for g in GROUPS:
                pe.wait_ge(prod_ready[g], T + 2)
            pe.wait_ge(logits_copied, T + BODY)
            logit(0, True).then_inc(logits_summed, 1)

            pe.wait_ge(id_ready, 1)
            for g in GROUPS:
                pe.wait_ge(zr_ready[g], T + 1)
            for n in range(N_COPY):
                part, m = n // BM, n % BM
                if m == 0:
                    pe.wait_ge(rows_loaded[part], DMA * HALVES)
                if n >= 4:
                    pe.wait_ge(turned_copied, n - 3)
                for k in range(PER_COPY):
                    last = nc.tensor.transpose(turn_bank(n)[:, k * P:(k + 1) * P],
                                               time_rows[:, part * PER_COPY + k, m * P:(m + 1) * P], ident[:])
                last.then_inc(turned, 1)
            for n in range(N_COPY):
                m, part = n // 2, n % 2
                pe.wait_ge(probs_ready, m + 1)
                if n >= 4:
                    pe.wait_ge((back_copied, back_copied_late)[part], m - 1)
                for k in range(PER_COPY):
                    last = nc.tensor.transpose(turn_bank(n)[:, k * P:(k + 1) * P],
                                               batch_rows[:, m, (part * PER_COPY + k) * P:(part * PER_COPY + k + 1) * P],
                                               ident[:])
                last.then_inc(back, 1)
            pe.wait_ge(back_copied, BM)
            pe.wait_ge(back_copied_late, BM)

            pe.wait_ge(split_done, 10)

            def add_bias(dst, part):
                return nc.tensor.matmul(dst, bias_split[:, part], ones[:], start=False, stop=False,
                                        skip_group_check=True)

            with pe.Fori(0, T, BODY) as t0:
                for s in range(BODY):
                    for g in GROUPS:
                        xs, hs = x_at(s)[:, gcols(g)], state[:, (s - 1) % 2, gcols(g)]
                        if g == 0 and s % CHUNK == 0:
                            pe.wait_ge(x_loaded[s // CHUNK], t0 + (T + DMA))
                        pe.wait_ge(ar_ready[g], t0 + (s + 1))
                        mm(r_bank[g][:, 0:GC], AX_R, xs, True, False)
                        add_bias(r_bank[g][:, 0:GC], 0)
                        pe.wait_ge(acand_ready[g][1], t0 + (s + 1))
                        last = mm(c_bank[g][:, GC:2 * GC], AX_C, xs, True, False)
                        if g == 1 and s % CHUNK == CHUNK - 1:
                            last.then_inc(x_used, CHUNK)
                        add_bias(c_bank[g][:, GC:2 * GC], 1)
                        pe.wait_ge(s_ready[g], t0 + (s + 1))
                        mm(r_bank[g][:, 0:GC], AH_R, hs, False, True).then_inc(ar_summed[g], 1)
                        mm(c_bank[g][:, 0:GC], AH_C, hs, False, True).then_inc(rc_summed[g], 1)


def kernel(r_keys, r_queries, L0_rec_W_att, L0_rec_gru_Wx, L0_rec_gru_Wh, L0_rec_gru_b_in, L0_rec_gru_b_rec,
           L0_rec_agru_Wx, L0_rec_agru_Wh, L0_rec_agru_b):
    import numpy as np
    import concourse.bacc as bacc
    from concourse.bass_utils import run_bass_kernel_spmd

    B, T, E = r_keys.shape
    half = B // 2
    keys = np.asarray(r_keys).reshape(2, half, T // CHUNK, CHUNK, E)
    arrays = {
        "keys_t": keys.transpose(2, 0, 4, 3, 1).reshape(T // CHUNK, 2 * E, CHUNK * half),
        "queries_t": np.asarray(r_queries).reshape(2, half, -1).transpose(0, 2, 1).reshape(-1, half),
        "weight_columns": np.concatenate([np.asarray(w) for w in (
            L0_rec_gru_Wx, L0_rec_gru_Wh, L0_rec_agru_Wx, L0_rec_agru_Wh, np.asarray(L0_rec_W_att).T)], axis=1),
        "bias_columns": np.concatenate([np.asarray(b).reshape(-1, E) for b in (
            L0_rec_gru_b_in, L0_rec_gru_b_rec, L0_rec_agru_b)]).T,
        "agru_b_row": np.tile(np.asarray(L0_rec_agru_b).reshape(1, 2, 1, E), (1, 1, 2, 1)).reshape(1, 2, 2 * E),
    }
    arrays = {k: np.ascontiguousarray(v) for k, v in arrays.items()}
    nc = bacc.Bacc("TRN2", target_bir_lowering=False, num_devices=1)
    args = [nc.dram_tensor(f"in_{k}", v.shape, F32, kind="ExternalInput").ap() for k, v in arrays.items()]
    out = nc.dram_tensor("out_state", (2 * E, half), F32, kind="ExternalOutput").ap()
    recurrent_attention_kernel(nc, *args, out)
    r = run_bass_kernel_spmd(nc, [{f"in_{k}": v for k, v in arrays.items()}], core_ids=[0])
    state = r.results[0]["out_state"]
    return np.ascontiguousarray(state.reshape(2, E, half).transpose(0, 2, 1).reshape(B, E))
```
